# Optimizing a Trainium2 kernel written in Bass

```python
import numpy as np
import jax
import jax.numpy as jnp

def _softmax(x, axis=-1):
    return jax.nn.softmax(x, axis=axis)

def _gelu(x):
    return jax.nn.gelu(x, approximate=True)

def _silu(x):
    return jax.nn.silu(x)

def _sigmoid(x):
    return jax.nn.sigmoid(x)

def _layernorm(x, axis=-1, eps=1e-05):
    m = jnp.mean(x, axis=axis, keepdims=True)
    v = jnp.var(x, axis=axis, keepdims=True)
    return (x - m) / jnp.sqrt(v + eps)

def _scatter_add(tgt, idx, src, axis=0):
    return tgt.at[idx].add(src)

def _segment_sum(src, seg, n):
    return jax.ops.segment_sum(src, seg, n)
kernel_name = 'mk_vit_tower_cls_d1_tok_img768_r4_a29214'

def setup_inputs(seed: int=0):
    np.random.seed(seed)
    _w = jnp.asarray

    def _rec_inputs():
        import jax
        import jax.numpy as jnp
        _rk = jax.random.key(seed)
        x = -0.000356955 + 1 * jax.random.normal(jax.random.fold_in(_rk, 1), (64, 3, 224, 224), jnp.float32)
        cls_tok = 0.02 * jax.random.normal(jax.random.fold_in(_rk, 5), (1, 1, 192), jnp.float32)
        return (x, cls_tok)
    x, cls_tok = _rec_inputs()

    def _L0_tok_setup():
        import jax, jax.numpy as jnp
        import numpy as np
        C, H, W = (3, 224, 224)
        P = 14
        PS = H // P
        PATCH_DIM = C * PS * PS
        HIDDEN = 192

        def patchify(images):
            n = images.shape[0]
            x = images.reshape(n, C, P, PS, P, PS)
            x = x.transpose(0, 2, 4, 1, 3, 5)
            return x.reshape(n, P * P, PATCH_DIM)
        key = jax.random.key(seed)
        k1, k2, k3 = jax.random.split(key, 3)
        images = jax.random.normal(k1, (128, C, H, W), dtype=jnp.float32)
        bound = 1.0 / np.sqrt(PATCH_DIM)
        W_lin = jax.random.uniform(k2, (HIDDEN, PATCH_DIM), minval=-bound, maxval=bound, dtype=jnp.float32)
        b_lin = jax.random.uniform(k3, (HIDDEN,), minval=-bound, maxval=bound, dtype=jnp.float32)
        cls_token = jnp.ones((1, HIDDEN), dtype=jnp.float32)
        return {'images': images, 'W_lin': W_lin, 'b_lin': b_lin, 'cls_token': cls_token}
    _L0_tok_all = _L0_tok_setup()
    _L0_tok_in = {k: v for k, v in _L0_tok_all.items() if k in ('W_lin', 'b_lin', 'cls_token')}
    del _L0_tok_all

    def _L0_attn_setup():
        import jax, jax.numpy as jnp
        import numpy as np
        EMBED_DIM = 192
        NUM_HEADS = 12
        HEAD_DIM = EMBED_DIM // NUM_HEADS
        SCALING = HEAD_DIM ** (-0.5)
        B, N = (4, 512)
        key = jax.random.key(seed)
        k_x, k_wqkv, k_bqkv, k_wo, k_bo = jax.random.split(key, 5)
        s = EMBED_DIM ** (-0.5)
        return {'x_q': jax.random.normal(k_x, (B, N, EMBED_DIM), dtype=jnp.float32), 'w_qkv': jax.random.normal(k_wqkv, (3 * EMBED_DIM, EMBED_DIM), dtype=jnp.float32) * s, 'b_qkv': jax.random.normal(k_bqkv, (3 * EMBED_DIM,), dtype=jnp.float32) * s, 'w_out': jax.random.normal(k_wo, (EMBED_DIM, EMBED_DIM), dtype=jnp.float32) * s, 'b_out': jax.random.normal(k_bo, (EMBED_DIM,), dtype=jnp.float32) * s}
    _L0_attn_all = _L0_attn_setup()
    _L0_attn_in = {k: v for k, v in _L0_attn_all.items() if k in ('w_qkv', 'b_qkv', 'w_out', 'b_out')}
    del _L0_attn_all

    def _L0_ffn_setup():
        import jax, jax.numpy as jnp
        import numpy as np
        E = 16
        D = 192
        K = D // 2
        SI = 2 * D
        B, N = (8, 1024)

        def _moe_mlp(x, gw, uw, dw):
            return jax.nn.silu(x @ gw) * (x @ uw) @ dw
        key = jax.random.key(seed)
        ks = jax.random.split(key, 20)
        s = lambda fan_in: 1.0 / np.sqrt(fan_in)
        inp = {}
        inp['hidden_states'] = jax.random.normal(ks[0], (B, N, D), jnp.float32)
        inp['posembed'] = jax.random.normal(ks[1], (E, D), jnp.float32)
        inp['pos_w'] = jax.random.uniform(ks[2], (D, D), jnp.float32, -s(D), s(D))
        inp['pos_b'] = jax.random.uniform(ks[3], (D,), jnp.float32, -s(D), s(D))
        inp['gate_w'] = jax.random.uniform(ks[4], (D, D), jnp.float32, -s(D), s(D))
        inp['gate_b'] = jax.random.uniform(ks[5], (D,), jnp.float32, -s(D), s(D))
        inp['eg_w'] = jax.random.uniform(ks[6], (E, K, D), jnp.float32, -s(K), s(K))
        inp['eu_w'] = jax.random.uniform(ks[7], (E, K, D), jnp.float32, -s(K), s(K))
        inp['ed_w'] = jax.random.uniform(ks[8], (E, D, D), jnp.float32, -s(D), s(D))
        inp['sg_w'] = jax.random.uniform(ks[9], (D, SI), jnp.float32, -s(D), s(D))
        inp['su_w'] = jax.random.uniform(ks[10], (D, SI), jnp.float32, -s(D), s(D))
        inp['sd_w'] = jax.random.uniform(ks[11], (SI, D), jnp.float32, -s(SI), s(SI))
        inp['ln_g'] = jnp.ones((D,), jnp.float32)
        inp['ln_b'] = jnp.zeros((D,), jnp.float32)
        inp['m1_w'] = jax.random.uniform(ks[12], (D, D), jnp.float32, -s(D), s(D))
        inp['m1_b'] = jax.random.uniform(ks[13], (D,), jnp.float32, -s(D), s(D))
        inp['m2_w'] = jax.random.uniform(ks[14], (D, D), jnp.float32, -s(D), s(D))
        inp['m2_b'] = jax.random.uniform(ks[15], (D,), jnp.float32, -s(D), s(D))
        return inp
    _L0_ffn_all = _L0_ffn_setup()
    _L0_ffn_in = {k: v for k, v in _L0_ffn_all.items() if k in ('posembed', 'pos_w', 'pos_b', 'gate_w', 'gate_b', 'eg_w', 'eu_w', 'ed_w', 'sg_w', 'su_w', 'sd_w', 'ln_g', 'ln_b', 'm1_w', 'm1_b', 'm2_w', 'm2_b')}
    del _L0_ffn_all
    return {'x': x, 'cls_tok': cls_tok, 'L0_tok_W_lin': _L0_tok_in['W_lin'], 'L0_tok_b_lin': _L0_tok_in['b_lin'], 'L0_tok_cls_token': _L0_tok_in['cls_token'], 'L0_attn_w_qkv': _L0_attn_in['w_qkv'], 'L0_attn_b_qkv': _L0_attn_in['b_qkv'], 'L0_attn_w_out': _L0_attn_in['w_out'], 'L0_attn_b_out': _L0_attn_in['b_out'], 'L0_ffn_posembed': _L0_ffn_in['posembed'], 'L0_ffn_pos_w': _L0_ffn_in['pos_w'], 'L0_ffn_pos_b': _L0_ffn_in['pos_b'], 'L0_ffn_gate_w': _L0_ffn_in['gate_w'], 'L0_ffn_gate_b': _L0_ffn_in['gate_b'], 'L0_ffn_eg_w': _L0_ffn_in['eg_w'], 'L0_ffn_eu_w': _L0_ffn_in['eu_w'], 'L0_ffn_ed_w': _L0_ffn_in['ed_w'], 'L0_ffn_sg_w': _L0_ffn_in['sg_w'], 'L0_ffn_su_w': _L0_ffn_in['su_w'], 'L0_ffn_sd_w': _L0_ffn_in['sd_w'], 'L0_ffn_ln_g': _L0_ffn_in['ln_g'], 'L0_ffn_ln_b': _L0_ffn_in['ln_b'], 'L0_ffn_m1_w': _L0_ffn_in['m1_w'], 'L0_ffn_m1_b': _L0_ffn_in['m1_b'], 'L0_ffn_m2_w': _L0_ffn_in['m2_w'], 'L0_ffn_m2_b': _L0_ffn_in['m2_b']}

def reference(x, cls_tok, L0_tok_W_lin, L0_tok_b_lin, L0_tok_cls_token, L0_attn_w_qkv, L0_attn_b_qkv, L0_attn_w_out, L0_attn_b_out, L0_ffn_posembed, L0_ffn_pos_w, L0_ffn_pos_b, L0_ffn_gate_w, L0_ffn_gate_b, L0_ffn_eg_w, L0_ffn_eu_w, L0_ffn_ed_w, L0_ffn_sg_w, L0_ffn_su_w, L0_ffn_sd_w, L0_ffn_ln_g, L0_ffn_ln_b, L0_ffn_m1_w, L0_ffn_m1_b, L0_ffn_m2_w, L0_ffn_m2_b):
    import jax
    import jax.numpy as jnp

    def _L0_tok_ref(images, W_lin, b_lin, cls_token):
        import jax, jax.numpy as jnp
        import numpy as np
        C, H, W = (3, 224, 224)
        P = 14
        PS = H // P
        PATCH_DIM = C * PS * PS
        HIDDEN = 192

        def patchify(images):
            n = images.shape[0]
            x = images.reshape(n, C, P, PS, P, PS)
            x = x.transpose(0, 2, 4, 1, 3, 5)
            return x.reshape(n, P * P, PATCH_DIM)
        patches = patchify(images)
        hidden = jnp.einsum('npd,hd->nph', patches, W_lin) + b_lin
        n = images.shape[0]
        cls = jnp.broadcast_to(cls_token[None], (n, 1, HIDDEN))
        return jnp.concatenate([cls, hidden], axis=1)

    def _L0_attn_ref(x_q, w_qkv, b_qkv, w_out, b_out):
        import jax, jax.numpy as jnp
        import numpy as np
        EMBED_DIM = 192
        NUM_HEADS = 12
        HEAD_DIM = EMBED_DIM // NUM_HEADS
        SCALING = HEAD_DIM ** (-0.5)
        B, N = (4, 512)
        b_sz, n, _ = x_q.shape
        qkv = jnp.einsum('bne,fe->bnf', x_q, w_qkv) + b_qkv
        qkv = qkv.reshape(b_sz, n, 3, NUM_HEADS, HEAD_DIM).transpose(0, 3, 2, 1, 4)
        q, k, v = (qkv[:, :, 0], qkv[:, :, 1], qkv[:, :, 2])
        q = q * SCALING
        attn = jnp.einsum('bhqd,bhkd->bhqk', q, k) + 1.0
        attn = jax.nn.softmax(attn, axis=-1)
        out = jnp.einsum('bhqk,bhkd->bhqd', attn, v)
        out = out.transpose(0, 2, 1, 3).reshape(b_sz, n, EMBED_DIM)
        return jnp.einsum('bne,fe->bnf', out, w_out) + b_out

    def _L0_ffn_ref(hidden_states, posembed, pos_w, pos_b, gate_w, gate_b, eg_w, eu_w, ed_w, sg_w, su_w, sd_w, ln_g, ln_b, m1_w, m1_b, m2_w, m2_b):
        import jax, jax.numpy as jnp
        import numpy as np
        E = 16
        D = 192
        K = D // 2
        SI = 2 * D
        B, N = (8, 1024)

        def _moe_mlp(x, gw, uw, dw):
            return jax.nn.silu(x @ gw) * (x @ uw) @ dw
        pe = jax.nn.softmax(posembed @ pos_w + pos_b, axis=-1)
        y = _moe_mlp(hidden_states, sg_w, su_w, sd_w)
        for i in range(E):
            gate_feature = hidden_states * pe[i] @ gate_w + gate_b
            gate_weight, gate_idx = jax.lax.top_k(gate_feature, K)
            gate_weight = jax.nn.softmax(gate_weight, axis=-1)
            gathered = jnp.take_along_axis(hidden_states, gate_idx, axis=-1)
            y = y + _moe_mlp(gathered * gate_weight, eg_w[i], eu_w[i], ed_w[i])
        mu = jnp.mean(y, axis=-1, keepdims=True)
        var = jnp.mean(jnp.square(y - mu), axis=-1, keepdims=True)
        yn = (y - mu) * jax.lax.rsqrt(var + 1e-06) * ln_g + ln_b
        return jax.nn.silu(yn @ m1_w + m1_b) @ m2_w + m2_b
    h = _L0_tok_ref(x, L0_tok_W_lin, L0_tok_b_lin, L0_tok_cls_token)
    h = jnp.concatenate([jnp.broadcast_to(cls_tok, (h.shape[0], 1, h.shape[2])), h], axis=1)
    h = h + _L0_attn_ref(_layernorm(h, axis=-1), L0_attn_w_qkv, L0_attn_b_qkv, L0_attn_w_out, L0_attn_b_out)
    h = h + _L0_ffn_ref(_layernorm(h, axis=-1), L0_ffn_posembed, L0_ffn_pos_w, L0_ffn_pos_b, L0_ffn_gate_w, L0_ffn_gate_b, L0_ffn_eg_w, L0_ffn_eu_w, L0_ffn_ed_w, L0_ffn_sg_w, L0_ffn_su_w, L0_ffn_sd_w, L0_ffn_ln_g, L0_ffn_ln_b, L0_ffn_m1_w, L0_ffn_m1_b, L0_ffn_m2_w, L0_ffn_m2_b)
    return h

_drawn_inputs = setup_inputs


def setup_inputs(seed=0):
    import zlib

    import numpy as np

    out = dict(_drawn_inputs(seed))
    spreads = {'L0_tok_cls_token': (1.0, 0.2), 'L0_ffn_ln_g': (1.0, 0.2), 'L0_ffn_ln_b': (0.0, 0.277)}
    factors = {'L0_ffn_posembed': 8.0,
     'L0_ffn_pos_w': 8.0,
     'L0_ffn_pos_b': 8.0,
     'L0_ffn_gate_w': 8.0,
     'L0_ffn_gate_b': 8.0,
     'L0_ffn_eg_w': 8.0,
     'L0_ffn_eu_w': 8.0,
     'L0_ffn_ed_w': 8.0,
     'L0_ffn_m1_b': 2.68}
    for name, (base, spread) in spreads.items():
        noise = np.random.default_rng([zlib.crc32(name.encode()), seed]).standard_normal(out[name].shape)
        drawn = base * np.exp(spread * noise) if base else spread * noise
        out[name] = jnp.asarray(drawn.astype(out[name].dtype))
    for name, factor in factors.items():
        out[name] = (out[name] * factor).astype(out[name].dtype)
    return out
```

```python
from contextlib import ExitStack

import numpy as np

import concourse.bass as bass
from concourse import mybir

F32 = mybir.dt.float32
BF16 = mybir.dt.bfloat16
U16 = mybir.dt.uint16
ALU = mybir.AluOpType
ACT = mybir.ActivationFunctionType
AX_X = mybir.AxisListType.X

IMAGES, SEQ, HALF = 64, 198, 99
D, DC = 192, 96
PATCH, PK = 768, 6
HEADS, HD = 12, 16
E, K = 16, 96
TOKENS = IMAGES * SEQ
TILES = TOKENS // 128
PAIRS = E // 2
GT, GH, GL = 8, 16, 12
GROUPS = 128 // GT
CHUNK = 4
CHUNKS = GROUPS // CHUNK
CT = CHUNK * GT
ROUNDS = K // 8
LOW = -3.0e38
MAGIC = 12582912.0


def constants():
    ident = np.eye(128, dtype=np.float32)
    spread = np.zeros((128, GROUPS // 2, 128), np.float32)
    for g in range(GROUPS // 2):
        for t in range(GT):
            for h in range(GH):
                spread[GT * g + t, g, t * GH + h] = -1.0
                spread[64 + GT * g + t, g, t * GH + h] = 2.0 * h
    hrow = np.zeros((128, 1), np.float32)
    for p in range(128):
        hrow[p, 0] = 1.0 - float(p % GH) ** 2
    sel = np.zeros((3, SEQ), np.float32)
    sel[0, 0] = 1.0
    sel[1, 1] = 1.0
    sel[2, 2:] = 1.0
    return ident, spread.reshape(128, GROUPS // 2 * 128), hrow, sel


def build(nc, a, out):
    with ExitStack() as ctx:
        def sb(name, shape, dt=F32):
            return ctx.enter_context(nc.sbuf_tensor(name, shape, dt))

        def sem(name):
            return ctx.enter_context(nc.semaphore(name))

        banks = [ctx.enter_context(nc.psum_tensor(f"bank{i}", [128, 512], F32)) for i in range(8)]
        h1 = nc.dram_tensor("h1_scratch", (TOKENS, D), F32, kind="Internal").ap()
        xs = nc.dram_tensor("xn_scratch", (TOKENS, D), F32, kind="Internal").ap()

        ident = sb("ident", [128, 128])
        identb = sb("identb", [128, 128], BF16)
        CAND = 2 * GL * 128
        space = sb("space", [128, 2 * CAND])
        zc = space[0:K, 0:CAND].rearrange("p (e l t) -> p e l t", e=2, l=GL)
        picked = space[0:K, CAND:2 * CAND].rearrange("p (e l t) -> p e l t", e=2, l=GL)
        spread32 = space[:, 0:GROUPS // 2 * 128]
        XIN = 2 * PK * SEQ
        xin = space[:, 1024:1024 + XIN].rearrange("p (b c s) -> p b c s", b=2, c=PK)
        eT = space[0:HALF, 1024 + XIN:1024 + XIN + 6 * SEQ].rearrange("p (b j s) -> p b j s", b=3, j=2)
        spread = sb("spread", [128, GROUPS // 2, 128], BF16)
        hrow = sb("hrow", [128, 1])
        sel = sb("sel", [3, SEQ])
        ones = sb("ones", [1, 128])
        w_patch = sb("w_patch", [128, PK, D])
        rows3 = sb("rows3", [3, D])
        w_qk = sb("w_qk", [DC, 2, 2, 3, 128])
        b_qk = sb("b_qk", [128, 2, 3])
        w_v = sb("w_v", [DC + 1, 2, D])
        w_o = sb("w_o", [DC + 1, 2, D])
        gatew = sb("gatew", [DC, 2, D])
        gates = sb("gates", [DC + 1, 2, E, D])
        egu = sb("egu", [DC, E, 2 * D])
        edn = sb("edn", [DC, 2, E, D])
        sgu = sb("sgu", [DC, 2, 2, 2 * D])
        sdn = sb("sdn", [DC, 2, 2, D])
        m1 = sb("m1", [DC, 2, D])
        m2 = sb("m2", [DC, 2, D])
        mb = sb("mb", [1, 2, D])
        lngb = sb("lngb", [DC, 2, 2])
        posT = sb("posT", [DC, 2, E])
        posw = sb("posw", [DC, 2, D])
        posb = sb("posb", [1, D])
        pe_sb = sb("pe_sb", [E, D])
        pe_st = sb("pe_st", [E, 4])
        peT = sb("peT", [DC, 2, E])

        loads = [
            (ident[:, :], a["ident"]), (spread32[:, :], a["spread"]), (hrow[:, :], a["hrow"]),
            (sel[:, :], a["sel"]),
            (w_patch[:, :, :], a["w_patch"]), (rows3[0:1, :], a["cls_tok"]),
            (rows3[1:2, :], a["tok_cls"]), (rows3[2:3, :], a["tok_b"]),
            (w_qk[:, :, :, :, :], a["w_qk"]), (b_qk[:, :, :], a["b_qk"]), (w_v[0:DC, :, :], a["w_v"]),
            (w_o[0:DC, :, :], a["w_o"]), (w_v[DC:DC + 1, 0, :], a["b_v"]), (w_o[DC:DC + 1, 0, :], a["b_o"]),
            (gatew[:, :, :], a["gate_w"]),
            (egu[:, :, 0:D], a["eg_w"]), (egu[:, :, D:2 * D], a["eu_w"]),
            (edn[:, 0, :, :], a["ed_w"][:, 0, :, :]), (edn[:, 1, :, :], a["ed_w"][:, 1, :, :]),
            (sgu[:, :, :, 0:D], a["sg_w"]), (sgu[:, :, :, D:2 * D], a["su_w"]),
            (sdn[:, :, :, :], a["sd_w"]), (m1[:, :, :], a["m1_w"]), (m2[:, :, :], a["m2_w"]),
            (mb[:, 0, :], a["m1_b"]), (mb[:, 1, :], a["m2_b"]),
            (lngb[:, 0, :], a["ln_g"]), (lngb[:, 1, :], a["ln_b"]),
            (posT[:, :, :], a["posT"]), (posw[:, :, :], a["pos_w"]), (posb[:, :], a["pos_b"]),
        ] + [(gates[DC:DC + 1, 0, i, :], a["gate_b"]) for i in range(E)]
        s_w = sem("weights_loaded")
        W_ALL = 16 * len(loads)

        h_sb = sb("h_sb", [HALF, 2, D])
        a_st = sb("a_st", [HALF, 2, 6])
        a_mv = sb("a_mv", [HALF, 2, 2])
        a_rs = sb("a_rs", [HALF, 2, 1])
        a_x = sb("a_x", [HALF, 2, D])
        a_xT = sb("a_xT", [DC + 1, 2, SEQ])
        qT = sb("qT", [128, 3, SEQ])
        q2T = sb("q2T", [128, 3, SEQ])
        kT = sb("kT", [128, 3, SEQ])
        vaug = sb("vaug", [HALF, 2, HEADS, HD + 1])
        mx = sb("mx", [HALF, 2, HEADS])
        mpad = sb("mpad", [HALF, 2, HEADS, 32])
        rc = sb("rc", [HALF, 2, HEADS])
        o_sb = sb("o_sb", [HALF, 2, D])
        oT = sb("oT", [DC + 1, 2, SEQ])
        hout = sb("hout", [HALF, 2, D])

        ht = sb("ht", [128, D])
        hres = sb("hres", [128, D])
        b_st = sb("b_st", [128, 6])
        b_mv = sb("b_mv", [128, 2])
        b_rs = sb("b_rs", [128, 1])
        xn = sb("xn", [128, D])
        xT = sb("xT", [DC + 1, 2, 128])
        xbd = sb("xbd", [128, GROUPS, GT, GL])
        gs = sb("gs", [128, 2, 2, D])
        left = sb("left", [128, 2, D])
        vals = sb("vals", [128, 2, 2, K])
        idx = sb("idx", [128, 2, 2, K], U16)
        nmax = sb("nmax", [128, 2, 1])
        ex = sb("ex", [128, 2, K])
        exs = sb("exs", [128, 2, 1])
        exr = sb("exr", [128, 2, 1])
        wn = sb("wn", [128, 2, K])
        hq = sb("hq", [128, 2, K])
        idf = sb("idf", [128, 2, K])
        hf = sb("hf", [128, 2, K])
        hl = sb("hl", [128, 2, K])
        lb = sb("lb", [128, 2, K], BF16)
        ab = sb("ab", [128, 2, 2, K], BF16)
        lT = sb("lT", [K, 2, 128], BF16)
        wT = sb("wT", [K, 2, 2, 128])
        mask = sb("mask", [K, GL, 2, 128], BF16)
        onehot = sb("onehot", [128, 4, CHUNK, K])
        gw = sb("gw", [K, 128])
        th = sb("th", [128, D])
        uh = sb("uh", [128, D])
        sg = sb("sg", [128, D])
        hid = sb("hid", [128, D])
        hT = sb("hT", [DC, 2, 128])
        y_st = sb("y_st", [128, 6])
        y_mv = sb("y_mv", [128, 2])
        y_rs = sb("y_rs", [128, 1])
        yz = sb("yz", [128, D])
        ot = sb("ot", [128, D])
        half_neg = sb("half_neg", [128, 2])

        block = ctx.enter_context(nc.Block())

        s_c = sem("constants_made")
        s_pp = sem("pe_logits")
        s_pm = sem("pe_max")
        s_px = sem("pe_exp")
        s_pn = sem("pe_normed")
        s_pt = sem("pe_turned")
        s_gw = sem("gates_made")
        s_lb = sem("ln_b_through_m1")
        s_m1 = sem("m1_folded")
        dch = sem("vector_chain")
        ach = sem("scalar_chain")
        pch = sem("pool_chain")
        dgo = sem("vector_started")
        pgo = sem("pool_started")
        s_hn = sem("half_neg_made")
        s_ve = sem("eps_added")
        sgo = sem("sync_started")
        s_xin = [sem("image_loaded0"), sem("image_loaded1")]
        sa_h = sem("a_hidden")
        sa_hc = sem("a_hidden_copied")
        sa_mv = sem("a_mean_var")
        sa_rs = sem("a_rstd")
        sa_x = sem("a_normed")
        sa_t = sem("a_turned")
        sa_xT = sem("a_xT")
        sa_qk = sem("a_qk")
        sa_v = sem("a_v")
        sa_q = sem("a_q_ready")
        sa_k = sem("a_k_ready")
        sa_va = sem("a_v_ready")
        sa_s = sem("a_scores")
        sa_mx = sem("a_max")
        sa_mp = sem("a_maxpad")
        sa_mt = sem("a_max_turned")
        sa_q2 = sem("a_q2_ready")
        sa_s2 = sem("a_scores_T")
        sa_e = sem("a_exp")
        sa_pv = sem("a_pv")
        sa_pva = sem("a_pv_all")
        sa_o = sem("a_o_ready")
        sa_ot = sem("a_o_turned")
        sa_oT = sem("a_oT")
        sa_y = sem("a_projected")
        sa_out = sem("a_out_ready")
        s_h1 = sem("h1_stored")
        s_ht = sem("tile_loaded")
        s_mv = sem("tile_mean_var")
        s_rs = sem("tile_rstd")
        s_ymv = sem("y_mean_var")
        s_yrs = sem("y_rstd")
        s_xn = sem("tile_normed")
        s_xs = sem("tile_normed_stored")
        s_xbd = sem("blockdiag_loaded")
        s_res = sem("residual_loaded")
        s_g = sem("gate_features")
        s_gs = sem("gate_features_copied")
        s_gu = sem("gate_features_used")
        s_so = sem("sorted")
        s_ex = sem("exp_done")
        s_wn = sem("weights_normed")
        s_h = sem("index_high")
        s_l = sem("index_low")
        s_ab = sem("high_shifted")
        s_aq = sem("high_in_place")
        s_wt = sem("weights_turned")
        s_lT = sem("low_T")
        s_wT = sem("weights_T")
        s_mk = sem("mask_ready")
        s_sp = sem("high_spread")
        s_oh = sem("onehot_ready")
        s_z = sem("candidates")
        s_zc = sem("candidates_copied")
        s_pk = sem("picked")
        s_ga = sem("gathered")
        s_gx = sem("gathered_weighted")
        s_e = sem("gate_up_done")
        s_th = sem("tanh_done")
        s_u = sem("up_copied")
        s_sg = sem("silu_done")
        s_hid = sem("hidden_done")
        s_tn = sem("turned")
        s_hT = sem("turned_copied")
        s_dn = sem("down_done")
        s_yz = sem("y_normed")
        s_m = sem("head_mlp_matmul")
        s_mt = sem("head_tanh")
        s_mh = sem("head_hidden")
        s_of = sem("out_ready")
        s_st = sem("out_stored")

        TURNS = 2 + E + 1 + 2

        def turn_no(t, pos):
            return t * TURNS + (1 + pos)

        def last_tile(t):
            return 1 if isinstance(t, int) and t == TILES - 1 else 0

        def numbers(t, q):
            late = 1 if isinstance(q, int) and q >= Q_NEXT and not last_tile(t) else 0
            P = t * PAIRS + q
            return P, P * 2, t * GATED + (q * 2 + 2), t * TURNS + (q * 2 + (3 + late))

        Q_NEXT = PAIRS - 2
        T_X = 2 + 2 * Q_NEXT
        T_Z, T_M = TURNS - 2, TURNS - 1
        GATED = 2 + E

        xin_v = a["x"]

        @block.sync
        def _(sp):
            for dst, src in loads:
                sp.dma_start(dst, src).then_inc(s_w, 16)

            def after(s, value):
                sp.wait_ge(s, value)
                sp.sem_inc(sgo, 1)

            def load_image(n, par):
                sp.dma_start(xin[:, par, :, :], xin_v[bass.ds(n, 1), :, :, :].rearrange(
                    "n p c s -> (n p) c s")).then_inc(s_xin[par], 16)

            load_image(0, 0)
            load_image(1, 1)

            def store_image(n, par, last):
                after(sa_out, n + 1)
                sp.dma_start(h1[bass.ds(n * SEQ, SEQ), :].rearrange("(j p) d -> p j d", j=2),
                             hout[:, :, :]).then_inc(s_h1, 16)
                if not last:
                    load_image(n + 2, par)

            with sp.Fori(0, IMAGES // 2 - 1) as m:
                store_image(m * 2, 0, False)
                store_image(m * 2 + 1, 1, False)
            store_image(IMAGES - 2, 0, True)
            store_image(IMAGES - 1, 1, True)
            sp.wait_ge(s_h1, 16 * IMAGES)

            def load_tile(t):
                sp.dma_start(ht[:, :], h1[bass.ds(t * 128, 128), :]).then_inc(s_ht, 16)

            def store_xn(t):
                after(s_xn, t + 1)
                sp.dma_start(xs[bass.ds(t * 128, 128), :], xn[:, :]).then_inc(s_xs, 16)
                after(s_xs, (t + 1) * 16)

            def load_blockdiag(t):
                v = xs[bass.ds(t * 128, 128), :].rearrange("(g t) (h l) -> h t g l", t=GT, h=GH)
                for i in range(GT):
                    sp.dma_start(xbd[GH * i:GH * i + GH, :, i, :], v[:, i, :, :]).then_inc(s_xbd, 16)

            def tile_end(t):
                after(s_of, t)
                sp.dma_start(hres[:, :], h1[bass.ds(t * 128, 128), :]).then_inc(s_res, 16)

            def store_out(t):
                after(s_of, t + 1)
                sp.dma_start(out[bass.ds(t * 128, 128), :], ot[:, :]).then_inc(s_st, 16)

            load_tile(0)
            store_xn(0)
            after(s_c, 1)
            load_blockdiag(0)
            load_tile(1)

            def step(t, more):
                tile_end(t)
                store_xn(t + 1)
                if more:
                    load_tile(t + 2)
                after(s_dn, (t + 1) * GATED)
                load_blockdiag(t + 1)
                store_out(t)

            with sp.Fori(0, TILES - 2) as t:
                step(t, True)
            step(TILES - 2, False)
            tile_end(TILES - 1)
            store_out(TILES - 1)
            sp.wait_ge(s_st, 16 * TILES)

        @block.tensor
        def _(pe):
            mm = nc.tensor.matmul
            tr = nc.tensor.transpose
            pe.wait_ge(s_w, W_ALL)
            pe.wait_ge(s_c, 1)
            mm(banks[0][0:E, 0:D], ones[:, 0:E], posb[:, :], start=True, stop=False)
            mm(banks[0][0:E, 0:D], posT[:, 0, :], posw[:, 0, :], start=False, stop=False)
            mm(banks[0][0:E, 0:D], posT[:, 1, :], posw[:, 1, :], start=False, stop=True).then_inc(s_pp, 1)
            mm(banks[1][0:1, 0:D], ones[:, 0:1], mb[:, 0, :], start=True, stop=False)
            mm(banks[1][0:1, 0:D], lngb[:, 1, 0:1], m1[:, 0, :], start=False, stop=False)
            mm(banks[1][0:1, 0:D], lngb[:, 1, 1:2], m1[:, 1, :], start=False, stop=True).then_inc(s_lb, 1)
            pe.wait_ge(s_pn, 1)
            for c in range(2):
                ins = tr(banks[2][0:DC, c * E:(c + 1) * E], pe_sb[:, c * DC:(c + 1) * DC], ident[0:E, 0:E])
            ins.then_inc(s_pt, 1)
            pe.wait_ge(s_gw, 1)

            def image(n, par, k):
                pe.wait_ge(s_xin[par], (k + 1) * 16)
                pe.wait_ge(sa_out, n)
                for j in range(2):
                    o = banks[0][0:HALF, j * D:(j + 1) * D]
                    mm(o, sel[:, j * HALF:(j + 1) * HALF], rows3[:, :], start=True, stop=False)
                    for c in range(PK):
                        ins = mm(o, xin[:, par, c, j * HALF:(j + 1) * HALF], w_patch[:, c, :],
                                 start=False, stop=(c == PK - 1))
                ins.then_inc(sa_h, 1)
                pe.wait_ge(sa_x, n * 2 + 2)
                for c in range(2):
                    for j in range(2):
                        ins = tr(banks[1][0:DC, (2 * c + j) * HALF:(2 * c + j + 1) * HALF],
                                 a_x[:, j, c * DC:(c + 1) * DC], ident[0:HALF, 0:HALF])
                ins.then_inc(sa_t, 1)
                pe.wait_ge(sa_xT, n + 1)
                for g in range(3):
                    for qk in range(2):
                        for c in range(2):
                            ins = mm(banks[2 + g][:, qk * SEQ:(qk + 1) * SEQ], w_qk[:, c, qk, g, :],
                                     a_xT[0:DC, c, :], start=(c == 0), stop=(c == 1))
                    ins.then_inc(sa_qk, 1)
                for j in range(2):
                    o = banks[0][0:HALF, j * D:(j + 1) * D]
                    for c in range(2):
                        r = DC + 1 - c
                        ins = mm(o, a_xT[0:r, c, j * HALF:(j + 1) * HALF], w_v[0:r, c, :],
                                 start=(c == 0), stop=(c == 1))
                ins.then_inc(sa_v, 1)
                pe.wait_ge(sa_q, n * 3 + 3)
                pe.wait_ge(sa_k, n * 3 + 3)
                for h in range(HEADS):
                    g, r = h // 4, 32 * (h % 4)
                    if h >= 4:
                        pe.wait_ge(sa_mx, n * HEADS + (h - 3))
                    for j in range(2):
                        ins = mm(banks[4 + h % 4][0:HALF, j * SEQ:(j + 1) * SEQ],
                                 qT[r:r + 32, g, j * HALF:(j + 1) * HALF], kT[r:r + 32, g, :],
                                 start=True, stop=True)
                    ins.then_inc(sa_s, 1)
                pe.wait_ge(sa_mp, n + 1)
                for g in range(3):
                    for j in range(2):
                        ins = tr(banks[2 + g // 2][:, (g % 2) * SEQ + j * HALF:(g % 2) * SEQ + (j + 1) * HALF],
                                 mpad[:, j, 4 * g:4 * g + 4, :].rearrange("p h w -> p (h w)"),
                                 ident[0:HALF, 0:HALF])
                ins.then_inc(sa_mt, 1)
                pe.wait_ge(sa_q2, n * 2 + 2)
                pe.wait_ge(sa_va, n + 1)

                def pv(h):
                    pe.wait_ge(sa_e, n * HEADS + (h + 1))
                    for jq in range(2):
                        o = banks[1][0:HALF, (jq * HEADS + h) * (HD + 1):(jq * HEADS + h + 1) * (HD + 1)]
                        for jk in range(2):
                            ins = mm(o, eT[:, h % 3, jk, jq * HALF:(jq + 1) * HALF], vaug[:, jk, h, :],
                                     start=(jk == 0), stop=(jk == 1))
                    ins.then_inc(sa_pv, 1)

                for h in range(HEADS):
                    g, r = h // 4, 32 * (h % 4)
                    if h >= 4:
                        pe.wait_ge(sa_e, n * HEADS + (h - 3))
                    for jk in range(2):
                        ins = mm(banks[4 + h % 4][0:HALF, jk * SEQ:(jk + 1) * SEQ],
                                 kT[r:r + 32, g, jk * HALF:(jk + 1) * HALF], q2T[r:r + 32, g, :],
                                 start=True, stop=True)
                    ins.then_inc(sa_s2, 1)
                    if h >= 1:
                        pv(h - 1)
                pv(HEADS - 1)
                pe.wait_ge(sa_o, n + 1)
                for c in range(2):
                    for j in range(2):
                        ins = tr(banks[2][0:DC, (2 * c + j) * HALF:(2 * c + j + 1) * HALF],
                                 o_sb[:, j, c * DC:(c + 1) * DC], ident[0:HALF, 0:HALF])
                ins.then_inc(sa_ot, 1)
                pe.wait_ge(sa_oT, n + 1)
                for j in range(2):
                    o = banks[0][0:HALF, j * D:(j + 1) * D]
                    for c in range(2):
                        r = DC + 1 - c
                        ins = mm(o, oT[0:r, c, j * HALF:(j + 1) * HALF], w_o[0:r, c, :],
                                 start=(c == 0), stop=(c == 1))
                ins.then_inc(sa_y, 1)

            with pe.Fori(0, IMAGES // 2) as m:
                image(m * 2, 0, m)
                image(m * 2 + 1, 1, m)
            pe.wait_ge(sa_out, IMAGES)

            def turn(no, src):
                pe.wait_ge(s_hT, no)
                for c in range(2):
                    ins = tr(banks[5][0:DC, 128 * c:128 * c + 128], src[:, c * DC:(c + 1) * DC], ident[:, :])
                ins.then_inc(s_tn, 1)

            def gate(P, q):
                if not isinstance(P, int) or P > 1:
                    pe.wait_ge(s_wT, P - 1)
                elif P == 1:
                    pe.wait_ge(s_gs, 1)
                o = banks[0][:, 0:2 * D]
                for c in range(2):
                    r = DC + 1 - c
                    ins = mm(o, xT[0:r, c, :], gates[0:r, c, bass.ds(q * 2, 2), :].rearrange("p a d -> p (a d)"),
                             start=(c == 0), stop=(c == 1))
                ins.then_inc(s_g, 1)

            def turn_index(P, copied):
                pe.wait_ge(s_l, P + 1)
                pe.wait_ge(s_wn, P * 2 + 2)
                pe.wait_ge(s_gs, copied)
                for e in range(2):
                    tr(banks[0][0:K, 384 + 64 * e:448 + 64 * e].bitcast(BF16), lb[:, e, :], identb[:, :])
                for e in range(2):
                    ins = tr(banks[0][0:K, 128 * e:128 * e + 128], wn[:, e, :], ident[:, :])
                ins.then_inc(s_wt, 1)

            def spread_chunk(P, j):
                e, c = j // CHUNKS, j % CHUNKS
                pe.wait_ge(s_oh, P * 2 * CHUNKS + max(j - 1, 0))
                for i in range(CHUNK):
                    g = (c * CHUNK + i) % (GROUPS // 2)
                    ins = mm(banks[1 + j % 2][:, i * K:(i + 1) * K], spread[:, g, :],
                             ab[:, c // (CHUNKS // 2), e, :], start=True, stop=True)
                ins.then_inc(s_sp, 1)

            def candidates(P, j):
                pe.wait_ge(s_oh, P * 2 * CHUNKS + (j + 1))
                pe.wait_ge(s_zc, P * 2 * CHUNKS + j)
                for i in range(CHUNK):
                    g = j % CHUNKS * CHUNK + i
                    ins = mm(banks[3 + j % 2][0:K, i * GT * GL:(i + 1) * GT * GL],
                             onehot[:, j % 4, i, :], xbd[:, g, :, :].rearrange("p t l -> p (t l)"),
                             start=True, stop=True)
                ins.then_inc(s_z, 1)

            def gather(P, j):
                if j == 0:
                    spread_chunk(P, 0)
                    spread_chunk(P, 1)
                if j + 2 < 2 * CHUNKS:
                    spread_chunk(P, j + 2)
                candidates(P, j)

            def pick(n, e):
                pe.wait_ge(s_pk, n * CHUNKS + CHUNKS)
                pe.wait_ge(s_gx, n)
                for l in range(GL):
                    ins = mm(banks[5][0:K, 384:512], ident[0:K, 0:K], picked[:, e, l, :],
                             start=(l == 0), stop=(l == GL - 1))
                ins.then_inc(s_ga, 1)

            def free_gated(w):
                pe.wait_ge(s_u, w)
                pe.wait_ge(s_sg, w)

            def expert_up(n, w, ex_):
                free_gated(w)
                pe.wait_ge(s_gx, n + 1)
                mm(banks[6][:, 0:2 * D], gw[:, :], egu[:, bass.ds(ex_, 1), :].rearrange("p a d -> p (a d)"),
                   start=True, stop=True).then_inc(s_e, 1)

            def down(no, weights, first=False, last=False):
                pe.wait_ge(s_hT, no + 1)
                for c in range(2):
                    ins = mm(banks[7][:, 0:D], hT[:, c, :], weights(c), start=(first and c == 0),
                             stop=(last and c == 1), skip_group_check=True)
                ins.then_inc(s_dn, 1)

            def shared(t):
                for half in range(2):
                    free_gated(t * GATED + half)
                    if half == 0:
                        pe.wait_ge(s_of, t)
                    for c in range(2):
                        ins = mm(banks[6][:, 0:2 * D], xT[0:DC, c, :], sgu[:, c, half, :],
                                 start=(c == 0), stop=(c == 1))
                    ins.then_inc(s_e, 1)
                    pe.wait_ge(s_hid, t * GATED + (half + 1))
                    turn(turn_no(t, half), hid)
                    down(turn_no(t, half), lambda c, half=half: sdn[:, half, c, :], first=(half == 0))

            def expert_down(u, ex_):
                down(u, lambda c: edn[:, c, bass.ds(ex_, 1), :].rearrange("p a d -> p (a d)"))

            def finish(t, q):
                P, n0, w0, u0 = numbers(t, q)
                expert_up(n0 + 1, w0 + 1, q * 2 + 1)
                pe.wait_ge(s_hid, w0 + 2)
                turn(u0 + 1, hid)
                expert_down(u0 + 1, q * 2 + 1)

            def pair(t, q, carry=True, ahead="same"):
                P, n0, w0, u0 = numbers(t, q)
                n1 = n0 + 1
                pe.wait_ge(s_ab, P * 3 + 3)
                pe.wait_ge(s_aq, P + 1)
                turn_index(P, P + 2 if ahead != "none" or (isinstance(q, int) and q == Q_NEXT) else P + 1)
                gather(P, 0)
                gather(P, 1)
                if carry:
                    _, np_, wp, up = numbers(t, q - 1)
                    expert_up(np_ + 1, wp + 1, q * 2 - 1)
                gather(P, 2)
                gather(P, 3)
                if carry:
                    pe.wait_ge(s_hid, wp + 2)
                    turn(up + 1, hid)
                gather(P, 4)
                if carry:
                    expert_down(up + 1, q * 2 - 1)
                if isinstance(q, int) and q == Q_NEXT and ahead == "next":
                    prepare(t + 1)
                gather(P, 5)
                pick(n0, 0)
                gather(P, 6)
                expert_up(n0, w0, q * 2)
                gather(P, 7)
                if ahead == "same":
                    gate(P + 2, q + 2)
                elif ahead == "next":
                    gate(P + 2, q - Q_NEXT)
                pe.wait_ge(s_hid, w0 + 1)
                turn(u0, hid)
                expert_down(u0, q * 2)
                pick(n1, 1)

            def prepare(t):
                pe.wait_ge(s_xn, t + 1)
                no = (t - 1) * TURNS + (1 + T_X) if not isinstance(t, int) or t > 0 else 0
                turn(no, xn)
                pe.wait_ge(s_hT, no + 1)

            def head(t):
                pe.wait_ge(s_yz, t + 1)
                turn(turn_no(t, T_Z - last_tile(t)), yz)
                free_gated((t + 1) * GATED)
                pe.wait_ge(s_hT, turn_no(t, T_Z - last_tile(t)) + 1)
                o = banks[6][:, 0:D]
                mm(o, ones[:, :], mb[:, 0, :], start=True, stop=False)
                for c in range(2):
                    ins = mm(o, hT[:, c, :], m1[:, c, :], start=False, stop=(c == 1))
                ins.then_inc(s_m, 1)
                pe.wait_ge(s_mh, t + 1)
                turn(turn_no(t, T_M - last_tile(t)), hid)
                pe.wait_ge(s_hT, turn_no(t, T_M - last_tile(t)) + 1)
                o = banks[6][:, D:2 * D]
                mm(o, ones[:, :], mb[:, 1, :], start=True, stop=False)
                for c in range(2):
                    ins = mm(o, hT[:, c, :], m2[:, c, :], start=False, stop=(c == 1))
                ins.then_inc(s_m, 1)

            prepare(0)
            gate(0, 0)
            gate(1, 1)

            def tile(t, last):
                shared(t)
                pe.wait_ge(s_xbd, (t + 1) * 16 * GT)
                pair(t, 0, carry=False)
                with pe.Fori(1, Q_NEXT) as q:
                    pair(t, q)
                pair(t, Q_NEXT, ahead="none" if last else "next")
                pair(t, PAIRS - 1, ahead="none" if last else "next")
                finish(t, PAIRS - 1)
                head(t)

            with pe.Fori(0, TILES - 1) as t:
                tile(t, False)
            tile(TILES - 1, True)

        @block.scalar
        def _(act):
            af = nc.scalar.activation
            act.wait_ge(s_w, W_ALL)
            act.wait_ge(s_pm, 1)
            af(pe_sb[:, :], banks[0][0:E, 0:D], ACT.Exp, bias=pe_st[:, 0:1],
               accum_out=pe_st[:, 1:2]).then_inc(s_px, 1)

            def image(n):
                act.wait_ge(sa_t, n + 1)
                af(a_xT[0:DC, :, :].rearrange("p c s -> p (c s)"), banks[1][0:DC, 0:2 * SEQ],
                   ACT.Copy).then_inc(sa_xT, 1)
                for g in range(3):
                    act.wait_ge(sa_q, n * 3 + (g + 1))
                    af(kT[:, g, :], banks[2 + g][:, SEQ:2 * SEQ], ACT.Identity,
                       bias=b_qk[:, 1, g:g + 1]).then_inc(sa_k, 1)
                for h in range(HEADS):
                    act.wait_ge(sa_s2, n * HEADS + (h + 1))
                    if h >= 3:
                        act.wait_ge(sa_pv, n * HEADS + (h - 2))
                    af(eT[:, h % 3, :, :].rearrange("p j s -> p (j s)"), banks[4 + h % 4][0:HALF, 0:2 * SEQ],
                       ACT.Exp, bias=1.0).then_inc(sa_e, 1)
                act.wait_ge(sa_ot, n + 1)
                af(oT[0:DC, :, :].rearrange("p c s -> p (c s)"), banks[2][0:DC, 0:2 * SEQ],
                   ACT.Copy).then_inc(sa_oT, 1)

            with act.Fori(0, IMAGES) as n:
                image(n)

            def turned(no, dst, scale=1.0):
                act.wait_ge(s_tn, no + 1)
                af(dst[0:DC, :, :].rearrange("p c s -> p (c s)"), banks[5][0:DC, 0:256], ACT.Copy,
                   scale=scale).then_inc(s_hT, 1)

            def gate(P, par):
                act.wait_ge(s_g, P + 1)
                act.wait_ge(s_gu, P + 1)
                af(gs[:, par, :, :].rearrange("p a d -> p (a d)"), banks[0][:, 0:2 * D],
                   ACT.Copy).then_inc(s_gs, 1)

            def exps(P, par):
                act.wait_ge(s_so, P + 1)
                af(nmax[:, :, :].rearrange("p e o -> p (e o)"), vals[:, par, :, 0], ACT.Copy,
                   scale=-1.0).then_inc(ach, 1)
                act.wait_ge(ach, 1)
                act.wait_ge(s_wn, P * 2)
                for e in range(2):
                    af(ex[:, e, :], vals[:, par, e, :], ACT.Exp, bias=nmax[:, e, :],
                       accum_out=exs[:, e, :]).then_inc(s_ex, 1)

            def squares(P):
                act.wait_ge(s_h, P + 1)
                af(ab[64:128, 0, :, :], hf[0:64, :, :], ACT.Copy).then_inc(s_ab, 1)
                af(ab[64:128, 1, :, :], hf[64:128, :, :], ACT.Copy).then_inc(s_ab, 1)
                af(ab[0:64, 1, :, :], hf[64:128, :, :], ACT.Square).then_inc(s_ab, 1)

            def index_turned(P, par):
                act.wait_ge(s_wt, P + 1)
                act.wait_ge(s_mk, P)
                af(lT[:, :, :].rearrange("p e t -> p (e t)"), banks[0][0:K, 384:512].bitcast(BF16),
                   ACT.Copy).then_inc(s_lT, 1)
                af(wT[:, par, :, :].rearrange("p e t -> p (e t)"), banks[0][0:K, 0:256],
                   ACT.Copy).then_inc(s_wT, 1)

            def onehots(P, j):
                act.wait_ge(s_sp, P * 2 * CHUNKS + (j + 1))
                if j >= 4:
                    act.wait_ge(s_z, P * 2 * CHUNKS + (j - 3))
                af(onehot[:, j % 4, :, :].rearrange("p i k -> p (i k)"), banks[1 + j % 2][:, 0:CHUNK * K],
                   ACT.Relu, bias=hrow[:, :]).then_inc(s_oh, 1)

            def copy_candidates(P, j):
                e, c = j // CHUNKS, j % CHUNKS
                act.wait_ge(s_z, P * 2 * CHUNKS + (j + 1))
                act.wait_ge(s_pk, P * 2 * CHUNKS)
                af(zc[:, e, :, CT * c:CT * c + CT].rearrange("p l t -> p t l"),
                   banks[3 + j % 2][0:K, 0:CT * GL].rearrange("p (t l) -> p t l", l=GL),
                   ACT.Copy).then_inc(s_zc, 1)

            def gated(w):
                act.wait_ge(s_e, w + 1)
                act.wait_ge(s_hid, w)
                af(th[:, :], banks[6][:, 0:D], ACT.Tanh, scale=0.5).then_inc(s_th, 1)
                af(uh[:, :], banks[6][:, D:2 * D], ACT.Copy, scale=0.5).then_inc(s_u, 1)

            def pair(t, q, par, carry=True, ahead="same"):
                P, n0, w0, u0 = numbers(t, q)
                n1 = n0 + 1
                act.sem_clear(ach)
                exps(P, par)
                squares(P)
                index_turned(P, par)
                onehots(P, 0)
                onehots(P, 1)
                for j in range(2 * CHUNKS):
                    if j + 2 < 2 * CHUNKS:
                        onehots(P, j + 2)
                    copy_candidates(P, j)
                    if j == 1 and carry:
                        gated(w0 - 1)
                    if j == 3 and carry:
                        turned(numbers(t, q - 1)[3] + 1, hT)
                    if j == 4 and isinstance(q, int) and q == Q_NEXT and ahead == "next":
                        turned(turn_no(t, T_X), xT)
                    if j == 6:
                        gated(w0)
                if ahead != "none":
                    gate(P + 2, par)
                turned(u0, hT)

            def shared(t):
                for half in range(2):
                    gated(t * GATED + half)
                    turned(turn_no(t, half), hT)

            def head(t):
                turned(turn_no(t, T_Z - last_tile(t)), hT)
                act.wait_ge(s_m, t * 2 + 1)
                af(th[:, :], banks[6][:, 0:D], ACT.Tanh, scale=0.5).then_inc(s_mt, 1)
                turned(turn_no(t, T_M - last_tile(t)), hT, scale=0.5)

            act.wait_ge(s_gw, 1)
            turned(0, xT)
            act.sem_inc(s_zc, 1)
            gate(0, 0)
            gate(1, 1)

            def tile(t, last):
                shared(t)
                pair(t, 0, 0, carry=False)
                with act.Fori(0, (Q_NEXT - 2) // 2) as i:
                    pair(t, i * 2 + 1, 1)
                    pair(t, i * 2 + 2, 0)
                pair(t, Q_NEXT - 1, 1)
                pair(t, Q_NEXT, 0, ahead="none" if last else "next")
                pair(t, PAIRS - 1, 1, ahead="none" if last else "next")
                gated(numbers(t, PAIRS - 1)[2] + 1)
                turned(numbers(t, PAIRS - 1)[3] + 1, hT)
                head(t)

            with act.Fori(0, TILES - 1) as t:
                tile(t, False)
            tile(TILES - 1, True)

        @block.gpsimd
        def _(pool):
            pl = nc.gpsimd

            def start(s, value):
                pool.wait_ge(s, value)
                pool.sem_inc(pgo, 1)

            def indices(P, par):
                start(s_so, P + 1)
                pl.tensor_scalar(idf[:, :, :], idx[:, par, :, :], 1.0, None, ALU.mult).then_inc(pch, 1)
                pool.wait_ge(pch, 1)
                pl.tensor_scalar(hq[:, :, :], idf[:, :, :], 1.0 / GL, -(GL - 1) / (2.0 * GL),
                                 ALU.mult, ALU.add).then_inc(pch, 1)
                pool.wait_ge(pch, 2)
                start(s_ab, P * 3)
                pl.tensor_scalar(hf[:, :, :], hq[:, :, :], MAGIC, MAGIC, ALU.add,
                                 ALU.subtract).then_inc(s_h, 1)
                start(s_h, P + 1)
                pl.tensor_scalar(hl[:, :, :], hf[:, :, :], -float(GL), None, ALU.mult).then_inc(pch, 1)
                pool.wait_ge(pch, 3)
                pool.wait_ge(s_wt, P)
                pl.tensor_tensor(lb[:, :, :], hl[:, :, :], idf[:, :, :], ALU.add).then_inc(s_l, 1)
                pool.wait_ge(s_sp, P * 2 * CHUNKS)
                pl.tensor_tensor(ab[0:64, 0, :, :], hf[0:64, :, :], hf[0:64, :, :], ALU.mult).then_inc(s_aq, 1)

            def pick(P, j):
                e, c = j // CHUNKS, j % CHUNKS
                pool.wait_ge(s_zc, P * 2 * CHUNKS + (j + 2))
                pool.wait_ge(s_ga, P * 2)
                pl.tensor_tensor(picked[:, e, :, CT * c:CT * c + CT], zc[:, e, :, CT * c:CT * c + CT],
                                 mask[:, :, e, CT * c:CT * c + CT], ALU.mult).then_inc(s_pk, 1)

            def hidden(w, no):
                pool.wait_ge(s_sg, w + 1)
                pool.wait_ge(s_u, w + 1)
                pool.wait_ge(s_tn, no)
                pl.tensor_tensor(hid[:, :], sg[:, :], uh[:, :], ALU.mult).then_inc(s_hid, 1)

            def pair(t, q, par, carry=True):
                P, n0, w0, u0 = numbers(t, q)
                pool.sem_clear(pch)
                indices(P, par)
                pool.wait_ge(s_mk, P + 1)
                for j in range(2 * CHUNKS):
                    pick(P, j)
                    if j == 2 and carry:
                        hidden(w0 - 1, numbers(t, q - 1)[3] + 1)
                    if j == 6:
                        hidden(w0, u0)

            pl.memset(half_neg[:, :], -0.5).then_inc(s_hn, 1)
            pool.wait_ge(s_hn, 1)

            def rstd(ready, count, dst, var, eps, made):
                start(ready, count)
                pool.sem_clear(s_ve)
                pl.tensor_scalar(dst, var, eps, None, ALU.add).then_inc(s_ve, 1)
                pool.wait_ge(s_ve, 1)
                pl.tensor_tensor(dst, dst, half_neg[0:dst.shape[0], 0:dst.shape[1]], ALU.pow).then_inc(made, 1)

            with pool.Fori(0, IMAGES) as n:
                rstd(sa_mv, n * 2 + 2, a_rs[:, :, 0], a_mv[:, :, 1], 1e-5, sa_rs)
            rstd(s_mv, 1, b_rs[:, :], b_mv[:, 1:2], 1e-5, s_rs)

            def tile(t, last):
                for half in range(2):
                    hidden(t * GATED + half, turn_no(t, half))
                if not last:
                    rstd(s_mv, t + 2, b_rs[:, :], b_mv[:, 1:2], 1e-5, s_rs)
                pair(t, 0, 0, carry=False)
                with pool.Fori(0, (Q_NEXT - 2) // 2) as i:
                    pair(t, i * 2 + 1, 1)
                    pair(t, i * 2 + 2, 0)
                pair(t, Q_NEXT - 1, 1)
                pair(t, Q_NEXT, 0)
                pair(t, PAIRS - 1, 1)
                _, _, w, u = numbers(t, PAIRS - 1)
                hidden(w + 1, u + 1)
                rstd(s_ymv, t + 1, y_rs[:, :], y_mv[:, 1:2], 1e-6, s_yrs)

            with pool.Fori(0, TILES - 1) as t:
                tile(t, False)
            tile(TILES - 1, True)

        @block.vector
        def _(dve):
            ve = nc.vector
            made = [0]

            def link(ins):
                made[0] += 1
                ins.then_inc(dch, 1)
                dve.wait_ge(dch, made[0])

            def new_chain():
                made[0] = 0
                dve.sem_clear(dch)

            def start(s, value):
                dve.wait_ge(s, value)
                dve.sem_inc(dgo, 1)

            link(ve.memset(xbd[:, :, :, :], 0.0))
            link(ve.memset(ones[:, :], 1.0))
            link(ve.memset(a_xT[DC:DC + 1, 0, :], 1.0))
            link(ve.memset(oT[DC:DC + 1, 0, :], 1.0))
            link(ve.memset(xT[DC:DC + 1, 0, :], 1.0))
            link(ve.memset(vaug[:, :, :, :], 1.0))
            link(ve.memset(mpad[:, :, :, :], 0.0))
            dve.wait_ge(s_w, W_ALL)
            link(ve.tensor_copy(identb[:, :], ident[:, :]))
            ve.tensor_copy(spread[:, :, :].rearrange("p g c -> p (g c)"), spread32[:, :]).then_inc(s_c, 1)
            dve.wait_ge(s_pp, 1)
            link(ve.tensor_reduce(pe_st[:, 2:3], banks[0][0:E, 0:D], AX_X, ALU.max))
            ve.tensor_scalar(pe_st[:, 0:1], pe_st[:, 2:3], -1.0, None, ALU.mult).then_inc(s_pm, 1)
            dve.wait_ge(s_px, 1)
            link(ve.reciprocal(pe_st[:, 3:4], pe_st[:, 1:2]))
            ve.tensor_scalar(pe_sb[:, :], pe_sb[:, :], pe_st[:, 3:4], None, ALU.mult).then_inc(s_pn, 1)
            dve.wait_ge(s_pt, 1)
            link(ve.tensor_copy(peT[:, :, :].rearrange("p c e -> p (c e)"), banks[2][0:DC, 0:2 * E]))
            for i in range(E):
                for c in range(2):
                    link(ve.tensor_scalar(gates[0:DC, c, i, :], gatew[:, c, :], peT[:, c, i:i + 1], None, ALU.mult))
            dve.wait_ge(s_lb, 1)
            link(ve.tensor_copy(mb[:, 0, :], banks[1][0:1, 0:D]))
            for c in range(2):
                link(ve.tensor_scalar(m1[:, c, :], m1[:, c, :], lngb[:, 0, c:c + 1], None, ALU.mult))
            dve.sem_inc(s_gw, 1)

            def image(n):
                new_chain()
                dve.wait_ge(sa_h, n + 1)
                link(ve.tensor_copy(h_sb[:, :, :].rearrange("p j d -> p (j d)"), banks[0][0:HALF, 0:2 * D]))
                for j in range(2):
                    link(ve.bn_stats(a_st[:, j, :], h_sb[:, j, :]))
                    ve.bn_aggr(a_mv[:, j, :], a_st[:, j, :]).then_inc(sa_mv, 1)
                dve.wait_ge(sa_rs, n + 1)
                for j in range(2):
                    ve.tensor_scalar(a_x[:, j, :], h_sb[:, j, :], a_mv[:, j, 0:1], a_rs[:, j, :],
                                     ALU.subtract, ALU.mult).then_inc(sa_x, 1)
                for g in range(3):
                    dve.wait_ge(sa_qk, n * 3 + (g + 1))
                    ve.tensor_scalar(qT[:, g, :], banks[2 + g][:, 0:SEQ], b_qk[:, 0, g:g + 1], HD ** -0.5,
                                     ALU.add, ALU.mult).then_inc(sa_q, 1)
                dve.wait_ge(sa_v, n + 1)
                ve.tensor_copy(vaug[:, :, :, 0:HD], banks[0][0:HALF, 0:2 * D].rearrange(
                    "p (j h d) -> p j h d", j=2, h=HEADS)).then_inc(sa_va, 1)
                for h in range(HEADS):
                    dve.wait_ge(sa_s, n * HEADS + (h + 1))
                    ve.tensor_reduce(mx[:, :, h:h + 1], banks[4 + h % 4][0:HALF, 0:2 * SEQ].rearrange(
                        "p (j s) -> p j s", j=2), AX_X, ALU.max).then_inc(sa_mx, 1)
                dve.wait_ge(sa_mx, n * HEADS + HEADS)
                ve.tensor_scalar(mpad[:, :, :, HD:HD + 1], mx[:, :, :].rearrange("p j (h o) -> p j h o", o=1),
                                 -1.0, -1.0, ALU.mult, ALU.add).then_inc(sa_mp, 1)
                dve.wait_ge(sa_mt, n + 1)
                ve.tensor_tensor(q2T[:, 0:2, :].rearrange("p g s -> p (g s)"), banks[2][:, 0:2 * SEQ],
                                 qT[:, 0:2, :].rearrange("p g s -> p (g s)"), ALU.add).then_inc(sa_q2, 1)
                ve.tensor_tensor(q2T[:, 2, :], banks[3][:, 0:SEQ], qT[:, 2, :], ALU.add).then_inc(sa_q2, 1)
                dve.wait_ge(sa_pv, n * HEADS + HEADS)
                ov = banks[1][0:HALF, 0:2 * HEADS * (HD + 1)].rearrange("p (j d) -> p j d", d=HD + 1)
                link(ve.reciprocal(rc[:, :, :].rearrange("p j (h o) -> p (j h) o", o=1), ov[:, :, HD:HD + 1]))
                ve.tensor_tensor(o_sb[:, :, :].rearrange("p j (h d) -> p (j h) d", d=HD), ov[:, :, 0:HD],
                                 rc[:, :, :].rearrange("p j (h o) -> p (j h) o", o=1).broadcast_to(
                                     [HALF, 2 * HEADS, HD]), ALU.mult).then_inc(sa_o, 1)
                dve.wait_ge(sa_y, n + 1)
                dve.wait_ge(s_h1, n * 16)
                ve.tensor_tensor(hout[:, :, :].rearrange("p j d -> p (j d)"), banks[0][0:HALF, 0:2 * D],
                                 h_sb[:, :, :].rearrange("p j d -> p (j d)"), ALU.add).then_inc(sa_out, 1)

            with dve.Fori(0, IMAGES) as n:
                image(n)

            def normalise(t):
                dve.wait_ge(s_ht, (t + 1) * 16)
                if not isinstance(t, int) or t > 0:
                    dve.wait_ge(s_xs, t * 16)
                link(ve.bn_stats(b_st[:, :], ht[:, :]))
                ve.bn_aggr(b_mv[:, :], b_st[:, :]).then_inc(s_mv, 1)
                dve.wait_ge(s_rs, t + 1)
                ve.tensor_scalar(xn[:, :], ht[:, :], b_mv[:, 0:1], b_rs[:, :],
                                 ALU.subtract, ALU.mult).then_inc(s_xn, 1)

            def weigh(P):
                dve.wait_ge(s_ex, P * 2 + 2)
                link(ve.reciprocal(exr[:, :, 0], exs[:, :, 0]))
                dve.wait_ge(s_wt, P)
                for e in range(2):
                    ve.tensor_scalar(wn[:, e, :], ex[:, e, :], exr[:, e, :], None, ALU.mult).then_inc(s_wn, 1)

            def masks(P):
                dve.wait_ge(s_lT, P + 1)
                dve.wait_ge(s_pk, P * 2 * CHUNKS)
                for l in range(GL):
                    ins = ve.tensor_scalar(mask[:, l, :, :], lT[:, :, :], float(l), None, ALU.is_equal)
                ins.then_inc(s_mk, 1)

            def gathered(n, e, par):
                dve.wait_ge(s_ga, n + 1)
                ve.tensor_tensor(gw[:, :], banks[5][0:K, 384:512], wT[:, par, e, :], ALU.mult).then_inc(s_gx, 1)

            def silu(w):
                dve.wait_ge(s_u, w + 1)
                dve.wait_ge(s_hid, w)
                ve.scalar_tensor_tensor(sg[:, :], th[:, :], 1.0, banks[6][:, 0:D], ALU.add,
                                        ALU.mult).then_inc(s_sg, 1)

            def sort(P, par, slots, first=False):
                new_chain()
                base = 0
                start(s_gs, P + 1)
                if not first:
                    start(s_ex, P * 2 - 2)
                    start(s_l, P - 1)
                for r in range(ROUNDS):
                    src = [gs[:, par, e, :] if r == 0 else left[:, e, :] for e in range(2)]
                    v = [vals[:, par, e, 8 * r:8 * r + 8] for e in range(2)]
                    for e in range(2):
                        if r:
                            dve.wait_ge(dch, replaced - 1 + e)
                        ve.max(v[e], src[e]).then_inc(dch, 1)
                    for e in range(2):
                        dve.wait_ge(dch, base + 1 + e)
                        ve.max_index(idx[:, par, e, 8 * r:8 * r + 8], v[e], src[e]).then_inc(dch, 1)
                    if r < ROUNDS - 1:
                        for e in range(2):
                            ins = ve.match_replace(left[:, e, :], v[e], src[e], LOW).then_inc(dch, 1)
                        base += 6
                        if r == 0:
                            dve.wait_ge(dch, base)
                            dve.sem_inc(s_gu, 1)
                    else:
                        base += 4
                        dve.wait_ge(dch, base)
                        dve.sem_inc(s_so, 1)
                    made[0] = base
                    replaced = base
                    for f in slots.get(r, ()):
                        f()
                    base = made[0]

            WEIGH, MASKS, GATHER1, SILU1, GATHER0, SILU0 = 0, 3, 2, 5, 9, 11

            def after(t, q, par, carry=True):
                P, n0, w0, _ = numbers(t, q)
                jobs = [(WEIGH, lambda: weigh(P)), (MASKS, lambda: masks(P)),
                        (GATHER0, lambda: gathered(n0, 0, par)), (SILU0, lambda: silu(w0))]
                if carry:
                    jobs += [(GATHER1, lambda: gathered(n0 - 1, 1, 1 - par)), (SILU1, lambda: silu(w0 - 1))]
                slots = {}
                for r, job in sorted(jobs, key=lambda x: x[0]):
                    slots.setdefault(r, []).append(job)
                return slots

            def shared(t):
                for half in range(2):
                    silu(t * GATED + half)

            def head(t):
                dve.wait_ge(s_dn, (t + 1) * GATED)
                link(ve.bn_stats(y_st[:, :], banks[7][:, 0:D]))
                ve.bn_aggr(y_mv[:, :], y_st[:, :]).then_inc(s_ymv, 1)
                dve.wait_ge(s_yrs, t + 1)
                ve.tensor_scalar(yz[:, :], banks[7][:, 0:D], y_mv[:, 0:1], y_rs[:, :],
                                 ALU.subtract, ALU.mult).then_inc(s_yz, 1)
                dve.wait_ge(s_mt, t + 1)
                dve.wait_ge(s_hid, (t + 1) * GATED)
                ve.scalar_tensor_tensor(hid[:, :], th[:, :], 1.0, banks[6][:, 0:D], ALU.add,
                                        ALU.mult).then_inc(s_mh, 1)
                dve.wait_ge(s_m, t * 2 + 2)
                dve.wait_ge(s_res, (t + 1) * 16)
                dve.wait_ge(s_st, t * 16)
                ve.tensor_tensor(ot[:, :], banks[6][:, D:2 * D], hres[:, :], ALU.add).then_inc(s_of, 1)

            new_chain()
            dve.sem_inc(s_gu, 2)
            normalise(0)
            sort(0, 0, {}, first=True)

            def tile(t, last):
                shared(t)
                P = t * PAIRS
                if not last:
                    new_chain()
                    normalise(t + 1)
                sort(P + 1, 1, after(t, 0, 0, carry=False))
                with dve.Fori(0, (Q_NEXT - 2) // 2) as i:
                    sort(P + i * 2 + 2, 0, after(t, i * 2 + 1, 1))
                    sort(P + i * 2 + 3, 1, after(t, i * 2 + 2, 0))
                sort(P + Q_NEXT, 0, after(t, Q_NEXT - 1, 1))
                sort(P + (PAIRS - 1), 1, after(t, Q_NEXT, 0))
                last_slots = after(t, PAIRS - 1, 1)
                if not last:
                    sort(P + PAIRS, 0, last_slots)
                else:
                    for r in sorted(last_slots):
                        for f in last_slots[r]:
                            f()
                _, n, w, _ = numbers(t, PAIRS - 1)
                gathered(n + 1, 1, 1)
                silu(w + 1)
                head(t)

            with dve.Fori(0, TILES - 1) as t:
                tile(t, False)
            tile(TILES - 1, True)



def kernel(x, cls_tok, **w):
    import concourse.bacc as bacc
    from concourse.bass_utils import run_bass_kernel_spmd

    def c(v):
        return np.ascontiguousarray(np.asarray(v))

    def chunked(v):
        v = np.asarray(v)
        return v.reshape((v.shape[0] // DC, DC) + v.shape[1:]).swapaxes(0, 1)

    def row(v):
        return np.asarray(v).reshape(1, D)

    t = {k[3:]: np.asarray(v) for k, v in w.items()}
    ident, spread, hrow, sel = constants()
    x = np.asarray(x).reshape(IMAGES, 3, 14, 16, 14, 16).transpose(0, 1, 3, 5, 2, 4).reshape(
        IMAGES, PK, 128, 196)
    xp = np.zeros((IMAGES, 128, PK, SEQ), np.float32)
    xp[:, :, :, 2:] = x.transpose(0, 2, 1, 3)
    wqkv, bqkv = t["attn_w_qkv"].reshape(3, HEADS, HD, D), t["attn_b_qkv"].reshape(3, HEADS, HD)
    wqk = np.zeros((2, HEADS, 32, D), np.float32)
    wqk[:, :, :HD] = wqkv[:2]
    bqk = np.zeros((2, HEADS, 32), np.float32)
    bqk[:, :, :HD] = bqkv[:2]
    bqk[1, :, HD] = 1.0
    arrays = {
        "x": xp, "ident": ident, "spread": spread, "hrow": hrow, "sel": sel,
        "cls_tok": row(cls_tok), "tok_cls": row(t["tok_cls_token"]), "tok_b": row(t["tok_b_lin"]),
        "w_patch": t["tok_W_lin"].T.reshape(PK, 128, D).transpose(1, 0, 2),
        "w_qk": chunked(wqk.reshape(2, 3, 128, D).transpose(3, 0, 1, 2)),
        "b_qk": bqk.reshape(2, 3, 128).transpose(2, 0, 1),
        "w_v": chunked(wqkv[2].reshape(D, D).T), "b_v": row(bqkv[2]),
        "w_o": chunked(t["attn_w_out"].T), "b_o": row(t["attn_b_out"]),
        "gate_w": chunked(t["ffn_gate_w"]), "gate_b": row(t["ffn_gate_b"]),
        "eg_w": t["ffn_eg_w"].transpose(1, 0, 2), "eu_w": t["ffn_eu_w"].transpose(1, 0, 2),
        "ed_w": t["ffn_ed_w"].reshape(E, 2, DC, D).transpose(2, 1, 0, 3),
        "sg_w": chunked(t["ffn_sg_w"].reshape(D, 2, D)), "su_w": chunked(t["ffn_su_w"].reshape(D, 2, D)),
        "sd_w": t["ffn_sd_w"].reshape(2, 2, DC, D).transpose(2, 0, 1, 3),
        "m1_w": chunked(t["ffn_m1_w"]), "m2_w": chunked(t["ffn_m2_w"]),
        "m1_b": row(t["ffn_m1_b"]), "m2_b": row(t["ffn_m2_b"]),
        "ln_g": chunked(t["ffn_ln_g"]), "ln_b": chunked(t["ffn_ln_b"]),
        "posT": chunked(t["ffn_posembed"].T), "pos_w": chunked(t["ffn_pos_w"]), "pos_b": row(t["ffn_pos_b"]),
    }
    nc = bacc.Bacc("TRN2", target_bir_lowering=False, num_devices=1)
    ins, aps = {}, {}
    for name, v in arrays.items():
        v = c(v)
        ins[f"in_{name}"] = v
        aps[name] = nc.dram_tensor(f"in_{name}", v.shape, mybir.dt.from_np(v.dtype), kind="ExternalInput").ap()
    out = nc.dram_tensor("out", (TOKENS, D), F32, kind="ExternalOutput").ap()
    build(nc, aps, out)
    r = run_bass_kernel_spmd(nc, [ins], core_ids=[0])
    return r.results[0]["out"].reshape(IMAGES, SEQ, D)
```

```python
from contextlib import ExitStack

import numpy as np

import concourse.bass as bass
from concourse import mybir

F32 = mybir.dt.float32
BF16 = mybir.dt.bfloat16
U16 = mybir.dt.uint16
ALU = mybir.AluOpType
ACT = mybir.ActivationFunctionType
AX_X = mybir.AxisListType.X

IMAGES, SEQ, HALF = 64, 198, 99
D, DC = 192, 96
PATCH, PK = 768, 6
HEADS, HD = 12, 16
E, K = 16, 96
TOKENS = IMAGES * SEQ
TILES = TOKENS // 128
PAIRS = E // 2
GT, GH, GL = 8, 16, 12
GROUPS = 128 // GT
CHUNK = 4
CHUNKS = GROUPS // CHUNK
CT = CHUNK * GT
ROUNDS = K // 8
LOW = -3.0e38
MAGIC = 12582912.0


def constants():
    ident = np.eye(128, dtype=np.float32)
    spread = np.zeros((128, GROUPS // 2, 128), np.float32)
    for g in range(GROUPS // 2):
        for t in range(GT):
            for h in range(GH):
                spread[GT * g + t, g, t * GH + h] = -1.0
                spread[64 + GT * g + t, g, t * GH + h] = 2.0 * h
    hrow = np.zeros((128, 1), np.float32)
    for p in range(128):
        hrow[p, 0] = 1.0 - float(p % GH) ** 2
    sel = np.zeros((3, SEQ), np.float32)
    sel[0, 0] = 1.0
    sel[1, 1] = 1.0
    sel[2, 2:] = 1.0
    return ident, spread.reshape(128, GROUPS // 2 * 128), hrow, sel


def build(nc, a, out):
    with ExitStack() as ctx:
        def sb(name, shape, dt=F32):
            return ctx.enter_context(nc.sbuf_tensor(name, shape, dt))

        def sem(name):
            return ctx.enter_context(nc.semaphore(name))

        banks = [ctx.enter_context(nc.psum_tensor(f"bank{i}", [128, 512], F32)) for i in range(8)]
        h1 = nc.dram_tensor("h1_scratch", (TOKENS, D), F32, kind="Internal").ap()
        xs = nc.dram_tensor("xn_scratch", (TOKENS, D), F32, kind="Internal").ap()

        ident = sb("ident", [128, 128])
        identb = sb("identb", [128, 128], BF16)
        CAND = 2 * GL * 128
        space = sb("space", [128, 2 * CAND])
        zc = space[0:K, 0:CAND].rearrange("p (e l t) -> p e l t", e=2, l=GL)
        picked = space[0:K, CAND:2 * CAND].rearrange("p (e l t) -> p e l t", e=2, l=GL)
        spread32 = space[:, 0:GROUPS // 2 * 128]
        XIN = 2 * PK * SEQ
        xin = space[:, 2 * CAND - XIN:2 * CAND].rearrange("p (b c s) -> p b c s", b=2, c=PK)
        eT = space[0:HALF, 0:16 * SEQ].rearrange("p (b j s) -> p b j s", b=8, j=2)
        spread = sb("spread", [128, GROUPS // 2, 128], BF16)
        hrow = sb("hrow", [128, 1])
        sel = sb("sel", [3, SEQ])
        ones = sb("ones", [1, 128])
        w_patch = sb("w_patch", [128, PK, D])
        rows3 = sb("rows3", [3, D])
        w_qk = sb("w_qk", [DC, 2, 2, 3, 128])
        b_qk = sb("b_qk", [128, 2, 3])
        w_v = sb("w_v", [DC + 1, 2, D])
        w_o = sb("w_o", [DC + 1, 2, D])
        gatew = sb("gatew", [DC, 2, D])
        gates = sb("gates", [DC + 1, 2, E, D])
        egu = sb("egu", [DC, E, 2 * D])
        edn = sb("edn", [DC, 2, E, D])
        sgu = sb("sgu", [DC, 2, 2, 2 * D])
        sdn = sb("sdn", [DC, 2, 2, D])
        m1 = sb("m1", [DC, 2, D])
        m2 = sb("m2", [DC, 2, D])
        mb = sb("mb", [1, 2, D])
        lngb = sb("lngb", [DC, 2, 2])
        posT = sb("posT", [DC, 2, E])
        posw = sb("posw", [DC, 2, D])
        posb = sb("posb", [1, D])
        pe_sb = sb("pe_sb", [E, D])
        pe_st = sb("pe_st", [E, 4])
        peT = sb("peT", [DC, 2, E])

        loads = [
            (ident[:, :], a["ident"]), (spread32[:, :], a["spread"]), (hrow[:, :], a["hrow"]),
            (sel[:, :], a["sel"]),
            (w_patch[:, :, :], a["w_patch"]), (rows3[0:1, :], a["cls_tok"]),
            (rows3[1:2, :], a["tok_cls"]), (rows3[2:3, :], a["tok_b"]),
            (w_qk[:, :, :, :, :], a["w_qk"]), (b_qk[:, :, :], a["b_qk"]), (w_v[0:DC, :, :], a["w_v"]),
            (w_o[0:DC, :, :], a["w_o"]), (w_v[DC:DC + 1, 0, :], a["b_v"]), (w_o[DC:DC + 1, 0, :], a["b_o"]),
            (gatew[:, :, :], a["gate_w"]),
            (egu[:, :, 0:D], a["eg_w"]), (egu[:, :, D:2 * D], a["eu_w"]),
            (edn[:, 0, :, :], a["ed_w"][:, 0, :, :]), (edn[:, 1, :, :], a["ed_w"][:, 1, :, :]),
            (sgu[:, :, :, 0:D], a["sg_w"]), (sgu[:, :, :, D:2 * D], a["su_w"]),
            (sdn[:, :, :, :], a["sd_w"]), (m1[:, :, :], a["m1_w"]), (m2[:, :, :], a["m2_w"]),
            (mb[:, 0, :], a["m1_b"]), (mb[:, 1, :], a["m2_b"]),
            (lngb[:, 0, :], a["ln_g"]), (lngb[:, 1, :], a["ln_b"]),
            (posT[:, :, :], a["posT"]), (posw[:, :, :], a["pos_w"]), (posb[:, :], a["pos_b"]),
        ] + [(gates[DC:DC + 1, 0, i, :], a["gate_b"]) for i in range(E)]
        s_w = sem("weights_loaded")
        W_ALL = 16 * len(loads)

        h_sb = sb("h_sb", [HALF, 2, D])
        a_st = sb("a_st", [HALF, 2, 6])
        a_mv = sb("a_mv", [HALF, 2, 2])
        a_rs = sb("a_rs", [HALF, 2, 1])
        a_x = sb("a_x", [HALF, 2, D])
        a_xT = sb("a_xT", [DC + 1, 2, SEQ])
        qT = sb("qT", [128, 3, SEQ])
        q2T = sb("q2T", [128, 3, SEQ])
        kT = sb("kT", [128, 3, SEQ])
        vaug = sb("vaug", [HALF, 2, HEADS, 32])
        mx = sb("mx", [HALF, 2, HEADS])
        mpad = sb("mpad", [HALF, 2, HEADS, 32])
        rc = sb("rc", [HALF, 2, HEADS])
        o_sb = sb("o_sb", [HALF, 2, D])
        oT = sb("oT", [DC + 1, 2, SEQ])
        hout = sb("hout", [HALF, 2, D])

        ht = sb("ht", [128, D])
        hres = sb("hres", [128, D])
        b_st = sb("b_st", [128, 6])
        b_mv = sb("b_mv", [128, 2])
        b_rs = sb("b_rs", [128, 1])
        xn = sb("xn", [128, D])
        xT = sb("xT", [DC + 1, 2, 128])
        xbd = sb("xbd", [128, GROUPS, GT, GL])
        gs = sb("gs", [128, 2, 2, D])
        left = sb("left", [128, 2, D])
        vals = sb("vals", [128, 2, 2, K])
        idx = sb("idx", [128, 2, 2, K], U16)
        nmax = sb("nmax", [128, 2, 1])
        ex = sb("ex", [128, 2, K])
        exs = sb("exs", [128, 2, 1])
        exr = sb("exr", [128, 2, 1])
        wn = sb("wn", [128, 2, K])
        hq = sb("hq", [128, 2, K])
        idf = sb("idf", [128, 2, K])
        hf = sb("hf", [128, 2, K])
        hl = sb("hl", [128, 2, K])
        lb = sb("lb", [128, 2, K], BF16)
        ab = sb("ab", [128, 2, 2, K], BF16)
        lT = sb("lT", [K, 2, 128], BF16)
        wT = sb("wT", [K, 2, 2, 128])
        mask = sb("mask", [K, GL, 2, 128], BF16)
        onehot = sb("onehot", [128, 4, CHUNK, K])
        gw = sb("gw", [K, 128])
        th = sb("th", [128, D])
        uh = sb("uh", [128, D])
        sg = sb("sg", [128, D])
        hid = sb("hid", [128, D])
        hT = sb("hT", [DC, 2, 128])
        zT = sb("zT", [DC, 2, 128])
        xS = sb("xS", [DC, 2, 128])
        y_st = sb("y_st", [128, 6])
        y_mv = sb("y_mv", [128, 2])
        y_rs = sb("y_rs", [128, 1])
        yz = sb("yz", [128, D])
        ot = sb("ot", [128, D])
        half_neg = sb("half_neg", [128, 2])

        block = ctx.enter_context(nc.Block())

        s_c = sem("constants_made")
        s_pp = sem("pe_logits")
        s_pm = sem("pe_max")
        s_px = sem("pe_exp")
        s_pn = sem("pe_normed")
        s_pt = sem("pe_turned")
        s_gw = sem("gates_made")
        s_lb = sem("ln_b_through_m1")
        s_m1 = sem("m1_folded")
        dch = sem("vector_chain")
        ach = sem("scalar_chain")
        pch = sem("pool_chain")
        dgo = sem("vector_started")
        pgo = sem("pool_started")
        s_hn = sem("half_neg_made")
        s_ve = sem("eps_added")
        sgo = sem("sync_started")
        s_xin = [sem("image_loaded0"), sem("image_loaded1")]
        sa_h = sem("a_hidden")
        sa_hc = sem("a_hidden_copied")
        sa_mv = sem("a_mean_var")
        sa_rs = sem("a_rstd")
        sa_x = sem("a_normed")
        sa_t = sem("a_turned")
        sa_xT = sem("a_xT")
        sa_qk = sem("a_qk")
        sa_v = sem("a_v")
        sa_q = sem("a_q_ready")
        sa_k = sem("a_k_ready")
        sa_va = sem("a_v_ready")
        sa_s = sem("a_scores")
        sa_mx = sem("a_max")
        sa_mp = sem("a_maxpad")
        sa_mt = sem("a_max_turned")
        sa_q2 = sem("a_q2_ready")
        sa_s2 = sem("a_scores_T")
        sa_e = sem("a_exp")
        sa_pv = sem("a_pv")
        sa_oq = sem("a_pv_copied")
        sa_ob = sem("a_pv_turned_back")
        sa_o = sem("a_o_ready")
        sa_ot = sem("a_o_turned")
        sa_oT = sem("a_oT")
        sa_y = sem("a_projected")
        sa_out = sem("a_out_ready")
        s_h1 = sem("h1_stored")
        s_ht = sem("tile_loaded")
        s_mv = sem("tile_mean_var")
        s_rs = sem("tile_rstd")
        s_ymv = sem("y_mean_var")
        s_yrs = sem("y_rstd")
        s_xn = sem("tile_normed")
        s_xs = sem("tile_normed_stored")
        s_xbd = sem("blockdiag_loaded")
        s_res = sem("residual_loaded")
        s_g = sem("gate_features")
        s_gs = sem("gate_features_copied")
        s_gu = sem("gate_features_used")
        s_so = sem("sorted")
        s_ex = sem("exp_done")
        s_wn = sem("weights_normed")
        s_h = sem("index_high")
        s_l = sem("index_low")
        s_ab = sem("high_shifted")
        s_aq = sem("high_in_place")
        s_wt = sem("weights_turned")
        s_lT = sem("low_T")
        s_wT = sem("weights_T")
        s_mk = sem("mask_ready")
        s_sp = sem("high_spread")
        s_oh = sem("onehot_ready")
        s_z = sem("candidates")
        s_zc = sem("candidates_copied")
        s_pk = sem("picked")
        s_ga = sem("gathered")
        s_gx = sem("gathered_weighted")
        s_e = sem("gate_up_done")
        s_th = sem("tanh_done")
        s_u = sem("up_copied")
        s_sg = sem("silu_done")
        s_hid = sem("hidden_done")
        s_tn = sem("turned")
        s_hT = sem("turned_copied")
        s_dn = sem("down_done")
        s_xS = sem("xT_kept")
        s_yz = sem("y_normed")
        s_m = sem("head_mlp_matmul")
        s_mt = sem("head_tanh")
        s_mh = sem("head_hidden")
        s_of = sem("out_ready")
        s_st = sem("out_stored")

        Q_NEXT, Q_HEAD = 6, PAIRS
        GATED = 2 + E
        TURNS = GATED + 3
        GATED_AT = {6: 8, 7: 11, 8: 14, 9: 16}
        TURNS_AT = {6: 8, 7: 12, 8: 15, 9: 18}

        def is_last(t):
            return isinstance(t, int) and t == TILES - 1

        def numbers(t, q):
            if t is None:
                return (q, (None, 2 * q - 1, 2 * q), (None, 2 * q, None, 2 * q + 1))
            P = t * PAIRS + q
            if not isinstance(q, int):
                w = t * GATED + (q * 2 - 1)
                u = t * TURNS + q * 2
                return P, (None, w, w + 1), (None, u, None, u + 1)
            if q < Q_NEXT:
                w0, u0 = 2 * q - 1, 2 * q
            else:
                w0, u0 = 3 + GATED_AT[q], 4 + TURNS_AT[q]
            if is_last(t) and q > Q_NEXT:
                u0 -= 1
            w, u = t * GATED + w0, t * TURNS + u0
            ew = 1 if q in (6, 7) else 0
            eu = 1 if q in (6, 7, 9) else 0
            mid = 1 if q == Q_HEAD or (q == Q_NEXT and not is_last(t)) else 0
            return (P, (w, w + ew, w + (ew + 1)),
                    (u, u + eu, u + (eu + 1), u + (eu + 1 + mid)))

        xin_v = a["x"]

        @block.sync
        def _(sp):
            for dst, src in loads:
                sp.dma_start(dst, src).then_inc(s_w, 16)

            def after(s, value):
                sp.wait_ge(s, value)
                sp.sem_inc(sgo, 1)

            def load_image(n, par):
                sp.dma_start(xin[:, par, :, :], xin_v[bass.ds(n, 1), :, :, :].rearrange(
                    "n p c s -> (n p) c s")).then_inc(s_xin[par], 16)

            load_image(0, 0)
            load_image(1, 1)

            def store_image(n, par, last):
                after(sa_out, n + 1)
                sp.dma_start(h1[bass.ds(n * SEQ, SEQ), :].rearrange("(j p) d -> p j d", j=2),
                             hout[:, :, :]).then_inc(s_h1, 16)
                if not last:
                    load_image(n + 2, par)

            with sp.Fori(0, IMAGES // 2 - 1) as m:
                store_image(m * 2, 0, False)
                store_image(m * 2 + 1, 1, False)
            store_image(IMAGES - 2, 0, True)
            store_image(IMAGES - 1, 1, True)
            sp.wait_ge(s_h1, 16 * IMAGES)

            def load_tile(t):
                sp.dma_start(ht[:, :], h1[bass.ds(t * 128, 128), :]).then_inc(s_ht, 16)

            def store_xn(t):
                after(s_xn, t + 1)
                sp.dma_start(xs[bass.ds(t * 128, 128), :], xn[:, :]).then_inc(s_xs, 16)
                after(s_xs, (t + 1) * 16)

            def load_blockdiag(t):
                v = xs[bass.ds(t * 128, 128), :].rearrange("(g t) (h l) -> h t g l", t=GT, h=GH)
                for i in range(GT):
                    sp.dma_start(xbd[GH * i:GH * i + GH, :, i, :], v[:, i, :, :]).then_inc(s_xbd, 16)

            def tile_end(t):
                after(s_of, t)
                sp.dma_start(hres[:, :], h1[bass.ds(t * 128, 128), :]).then_inc(s_res, 16)

            def store_out(t):
                after(s_of, t + 1)
                sp.dma_start(out[bass.ds(t * 128, 128), :], ot[:, :]).then_inc(s_st, 16)

            load_tile(0)
            store_xn(0)
            after(s_c, 1)
            load_blockdiag(0)
            load_tile(1)

            def step(t, more):
                tile_end(t)
                store_xn(t + 1)
                if more:
                    load_tile(t + 2)
                after(s_z, (t + 1) * (PAIRS * 2 * CHUNKS))
                load_blockdiag(t + 1)
                store_out(t)

            with sp.Fori(0, TILES - 2) as t:
                step(t, True)
            step(TILES - 2, False)
            tile_end(TILES - 1)
            store_out(TILES - 1)
            sp.wait_ge(s_st, 16 * TILES)

        @block.tensor
        def _(pe):
            mm = nc.tensor.matmul
            tr = nc.tensor.transpose
            pe.wait_ge(s_w, W_ALL)
            pe.wait_ge(s_c, 1)
            mm(banks[0][0:E, 0:D], ones[:, 0:E], posb[:, :], start=True, stop=False)
            mm(banks[0][0:E, 0:D], posT[:, 0, :], posw[:, 0, :], start=False, stop=False)
            mm(banks[0][0:E, 0:D], posT[:, 1, :], posw[:, 1, :], start=False, stop=True).then_inc(s_pp, 1)
            mm(banks[1][0:1, 0:D], ones[:, 0:1], mb[:, 0, :], start=True, stop=False)
            mm(banks[1][0:1, 0:D], lngb[:, 1, 0:1], m1[:, 0, :], start=False, stop=False)
            mm(banks[1][0:1, 0:D], lngb[:, 1, 1:2], m1[:, 1, :], start=False, stop=True).then_inc(s_lb, 1)
            pe.wait_ge(s_pn, 1)
            for c in range(2):
                ins = tr(banks[2][0:DC, c * E:(c + 1) * E], pe_sb[:, c * DC:(c + 1) * DC], ident[0:E, 0:E])
            ins.then_inc(s_pt, 1)
            pe.wait_ge(s_gw, 1)

            def image(n, par, k):
                pe.wait_ge(s_xin[par], (k + 1) * 16)
                pe.wait_ge(sa_out, n)
                for j in range(2):
                    o = banks[0][0:HALF, j * D:(j + 1) * D]
                    mm(o, sel[:, j * HALF:(j + 1) * HALF], rows3[:, :], start=True, stop=False)
                    for c in range(PK):
                        ins = mm(o, xin[:, par, c, j * HALF:(j + 1) * HALF], w_patch[:, c, :],
                                 start=False, stop=(c == PK - 1))
                ins.then_inc(sa_h, 1)
                pe.wait_ge(sa_x, n * 2 + 2)
                for c in range(2):
                    for j in range(2):
                        ins = tr(banks[1][0:DC, (2 * c + j) * HALF:(2 * c + j + 1) * HALF],
                                 a_x[:, j, c * DC:(c + 1) * DC], ident[0:HALF, 0:HALF])
                ins.then_inc(sa_t, 1)
                pe.wait_ge(sa_xT, n + 1)
                for g in range(3):
                    for qk in range(2):
                        for c in range(2):
                            ins = mm(banks[2 + g][:, qk * SEQ:(qk + 1) * SEQ], w_qk[:, c, qk, g, :],
                                     a_xT[0:DC, c, :], start=(c == 0), stop=(c == 1))
                    ins.then_inc(sa_qk, 1)
                for j in range(2):
                    o = banks[0][0:HALF, j * D:(j + 1) * D]
                    for c in range(2):
                        r = DC + 1 - c
                        ins = mm(o, a_xT[0:r, c, j * HALF:(j + 1) * HALF], w_v[0:r, c, :],
                                 start=(c == 0), stop=(c == 1))
                ins.then_inc(sa_v, 1)
                pe.wait_ge(sa_q, n * 3 + 3)
                pe.wait_ge(sa_k, n * 3 + 3)
                for g in range(3):
                    for j in range(2):
                        for i in range(4):
                            if g and j == 0:
                                pe.wait_ge(sa_mx, n * HEADS + (4 * g - 3 + i))
                            r = 32 * i
                            ins = mm(banks[4 + i][0:HALF, j * SEQ:(j + 1) * SEQ],
                                     qT[r:r + 32, g, j * HALF:(j + 1) * HALF], kT[r:r + 32, g, :],
                                     start=True, stop=True)
                            if j:
                                ins.then_inc(sa_s, 1)
                pe.wait_ge(sa_mp, n + 1)
                for g in range(3):
                    for j in range(2):
                        ins = tr(banks[2 + g // 2][:, (g % 2) * SEQ + j * HALF:(g % 2) * SEQ + (j + 1) * HALF],
                                 mpad[:, j, 4 * g:4 * g + 4, :].rearrange("p h w -> p (h w)"),
                                 ident[0:HALF, 0:HALF])
                ins.then_inc(sa_mt, 1)
                pe.wait_ge(sa_q2, n * 2 + 2)
                pe.wait_ge(sa_va, n + 1)

                def scores_T(g):
                    for jk in range(2):
                        for i in range(4):
                            if g and jk == 0:
                                pe.wait_ge(sa_e, n * HEADS + (4 * g - 3 + i))
                            r = 32 * i
                            ins = mm(banks[4 + i][0:HALF, jk * SEQ:(jk + 1) * SEQ],
                                     kT[r:r + 32, g, jk * HALF:(jk + 1) * HALF], q2T[r:r + 32, g, :],
                                     start=True, stop=True)
                            if jk:
                                ins.then_inc(sa_s2, 1)

                def pv(g):
                    pe.wait_ge(sa_e, n * HEADS + 4 * (g + 1))
                    for jk in range(2):
                        for i in range(4):
                            h, r = 4 * g + i, 32 * i
                            ins = mm(banks[1 + g][r:r + 32, 0:SEQ], vaug[:, jk, h, :], eT[:, h % 8, jk, :],
                                     start=(jk == 0), stop=(jk == 1), tile_position=(0, r))
                    ins.then_inc(sa_pv, 1)

                scores_T(0)
                scores_T(1)
                pv(0)
                scores_T(2)
                pv(1)
                pv(2)
                pe.wait_ge(sa_oq, n * 3 + 3)
                for j in range(2):
                    for g in range(3):
                        ins = tr(banks[4 + j][0:HALF, g * 128:(g + 1) * 128],
                                 qT[:, g, j * HALF:(j + 1) * HALF], ident[:, :])
                    ins.then_inc(sa_ob, 1)
                pe.wait_ge(sa_o, n * 2 + 2)
                for c in range(2):
                    for j in range(2):
                        ins = tr(banks[2][0:DC, (2 * c + j) * HALF:(2 * c + j + 1) * HALF],
                                 o_sb[:, j, c * DC:(c + 1) * DC], ident[0:HALF, 0:HALF])
                ins.then_inc(sa_ot, 1)
                pe.wait_ge(sa_oT, n + 1)
                for j in range(2):
                    o = banks[0][0:HALF, j * D:(j + 1) * D]
                    for c in range(2):
                        r = DC + 1 - c
                        ins = mm(o, oT[0:r, c, j * HALF:(j + 1) * HALF], w_o[0:r, c, :],
                                 start=(c == 0), stop=(c == 1))
                ins.then_inc(sa_y, 1)

            with pe.Fori(0, IMAGES // 2) as m:
                image(m * 2, 0, m)
                image(m * 2 + 1, 1, m)
            pe.wait_ge(sa_out, IMAGES)

            def turn(no, src):
                pe.wait_ge(s_hT, no)
                for c in range(2):
                    ins = tr(banks[5][0:DC, 128 * c:128 * c + 128], src[:, c * DC:(c + 1) * DC], ident[:, :])
                ins.then_inc(s_tn, 1)

            def gate(P, q):
                if not isinstance(P, int) or P > 1:
                    pe.wait_ge(s_wT, P - 1)
                elif P == 1:
                    pe.wait_ge(s_gs, 1)
                o = banks[0][:, 0:2 * D]
                for c in range(2):
                    r = DC + 1 - c
                    ins = mm(o, xT[0:r, c, :], gates[0:r, c, bass.ds(q * 2, 2), :].rearrange("p a d -> p (a d)"),
                             start=(c == 0), stop=(c == 1))
                ins.then_inc(s_g, 1)

            def turn_index(P, copied):
                pe.wait_ge(s_l, P + 1)
                pe.wait_ge(s_wn, P * 2 + 2)
                pe.wait_ge(s_gs, copied)
                for e in range(2):
                    tr(banks[0][0:K, 384 + 64 * e:448 + 64 * e].bitcast(BF16), lb[:, e, :], identb[:, :])
                for e in range(2):
                    ins = tr(banks[0][0:K, 128 * e:128 * e + 128], wn[:, e, :], ident[:, :])
                ins.then_inc(s_wt, 1)

            def spread_chunk(P, j):
                e, c = j // CHUNKS, j % CHUNKS
                pe.wait_ge(s_oh, P * 2 * CHUNKS + max(j - 1, 0))
                for i in range(CHUNK):
                    g = (c * CHUNK + i) % (GROUPS // 2)
                    ins = mm(banks[1 + j % 2][:, i * K:(i + 1) * K], spread[:, g, :],
                             ab[:, c // (CHUNKS // 2), e, :], start=True, stop=True)
                ins.then_inc(s_sp, 1)

            def candidates(P, j):
                pe.wait_ge(s_oh, P * 2 * CHUNKS + (j + 1))
                pe.wait_ge(s_zc, P * 2 * CHUNKS + j)
                for i in range(CHUNK):
                    g = j % CHUNKS * CHUNK + i
                    ins = mm(banks[3 + j % 2][0:K, i * GT * GL:(i + 1) * GT * GL],
                             onehot[:, j % 4, i, :], xbd[:, g, :, :].rearrange("p t l -> p (t l)"),
                             start=True, stop=True)
                ins.then_inc(s_z, 1)

            def gather(P, j):
                if j == 0:
                    spread_chunk(P, 0)
                    spread_chunk(P, 1)
                if j + 2 < 2 * CHUNKS:
                    spread_chunk(P, j + 2)
                candidates(P, j)

            def pick(n, e, w):
                pe.wait_ge(s_pk, n * CHUNKS + CHUNKS)
                free_gated(w)
                for l in range(GL):
                    ins = mm(banks[6][0:K, 2 * D:2 * D + 128], ident[0:K, 0:K], picked[:, e, l, :],
                             start=(l == 0), stop=(l == GL - 1))
                ins.then_inc(s_ga, 1)

            def free_gated(w):
                pe.wait_ge(s_u, w)
                pe.wait_ge(s_sg, w)

            def expert_up(n, w, ex_):
                free_gated(w)
                pe.wait_ge(s_gx, n + 1)
                mm(banks[6][:, 0:2 * D], gw[:, :], egu[:, bass.ds(ex_, 1), :].rearrange("p a d -> p (a d)"),
                   start=True, stop=True).then_inc(s_e, 1)

            def down(no, weights, first=False, last=False):
                pe.wait_ge(s_hT, no + 1)
                for c in range(2):
                    ins = mm(banks[7][:, 0:D], hT[:, c, :], weights(c), start=(first and c == 0),
                             stop=(last and c == 1), skip_group_check=True)
                ins.then_inc(s_dn, 1)

            def expert_down(u, ex_, first=False):
                down(u, lambda c: edn[:, c, bass.ds(ex_, 1), :].rearrange("p a d -> p (a d)"), first)

            def shared_up(t, half, w):
                free_gated(w)
                if half:
                    pe.wait_ge(s_xS, t + 1)
                src = xS if half else xT
                for c in range(2):
                    ins = mm(banks[6][:, 0:2 * D], src[0:DC, c, :], sgu[:, c, half, :],
                             start=(c == 0), stop=(c == 1))
                ins.then_inc(s_e, 1)

            def head_linear(src, row, weights, cols):
                mm(banks[6][:, cols:cols + D], ones[:, :], mb[:, row, :], start=True, stop=False)
                for c in range(2):
                    ins = mm(banks[6][:, cols:cols + D], src[:, c, :], weights[:, c, :], start=False, stop=(c == 1))
                ins.then_inc(s_m, 1)

            def head_first(t, w, u):
                free_gated(w)
                pe.wait_ge(s_hT, u + 1)
                head_linear(zT, 0, m1, 0)

            def head_turn(t, u):
                pe.wait_ge(s_mh, t + 1)
                turn(u, hid)

            def head_second(u):
                pe.wait_ge(s_hT, u + 1)
                head_linear(hT, 1, m2, D)

            def pair(t, q, ex_=None):
                P, (wx, wc, wo), (ux, uc, um, uo) = numbers(t, q)
                n0 = P * 2
                qi = q if isinstance(q, int) else None
                first_pair = t is None and q == 0
                ex_ = q * 2 if ex_ is None else ex_
                exc = E - 1 if qi == Q_HEAD else ex_ - 1
                half = {6: 0, 7: 1}.get(qi) if t is not None else None
                head_2 = qi == Q_HEAD + 1 and t is not None
                plain = half is None and not head_2 and not first_pair
                ahead = not (is_last(t) and qi in (6, 7))
                if not first_pair:
                    pe.wait_ge(s_gx, n0)
                if half is not None:
                    shared_up(t, half, wx)
                if head_2:
                    head_first(t, wc, numbers(t, 8)[2][2])
                if plain:
                    expert_up(n0 - 1, wc, exc)
                pe.wait_ge(s_ab, P * 3 + 3)
                pe.wait_ge(s_aq, P + 1)
                turn_index(P, P + 2 if ahead or qi == 6 else P + 1)
                if qi == Q_HEAD and t is not None:
                    pe.wait_ge(s_xbd, (t + 2) * 16 * GT)
                gather(P, 0)
                gather(P, 1)
                if half is not None:
                    pe.wait_ge(s_hid, wx + 1)
                    turn(ux, hid)
                    expert_up(n0 - 1, wc, exc)
                if head_2:
                    head_turn(t, ux)
                if plain:
                    pe.wait_ge(s_hid, wc + 1)
                    turn(uc, hid)
                gather(P, 2)
                if half is not None:
                    down(ux, lambda c: sdn[:, half, c, :])
                if head_2:
                    head_second(ux)
                if plain:
                    expert_down(uc, exc)
                gather(P, 3)
                if head_2:
                    pe.wait_ge(s_of, t + 1)
                    expert_up(n0 - 1, wc, exc)
                gather(P, 4)
                if half is not None:
                    pe.wait_ge(s_hid, wc + 1)
                    turn(uc, hid)
                gather(P, 5)
                if half is not None:
                    expert_down(uc, exc)
                if head_2:
                    pe.wait_ge(s_hid, wc + 1)
                    turn(uc, hid)
                if qi == Q_NEXT and ahead:
                    pe.wait_ge(s_xn, t + 2)
                    pe.wait_ge(s_xS, t + 1)
                    turn(um, xn)
                pick(n0, 0, wo)
                gather(P, 6)
                if head_2:
                    expert_down(uc, exc)
                if qi == Q_HEAD and t is not None:
                    pe.wait_ge(s_yz, t + 1)
                    turn(um, yz)
                expert_up(n0, wo, ex_)
                gather(P, 7)
                if qi == Q_NEXT and ahead:
                    pe.wait_ge(s_hT, um + 1)
                if ahead:
                    gate(P + 2, q + 2 if qi is None or q < Q_NEXT else q + 2 - PAIRS)
                pe.wait_ge(s_hid, wo + 1)
                turn(uo, hid)
                pick(n0 + 1, 1, wo + 1)
                expert_down(uo, ex_, first=(first_pair or (qi == Q_HEAD and t is not None)))

            pe.wait_ge(s_xn, 1)
            turn(0, xn)
            pe.wait_ge(s_hT, 1)
            gate(0, 0)
            gate(1, 1)
            pe.wait_ge(s_xbd, 16 * GT)
            pair(None, 0)
            pair(None, 1)

            def tile(t):
                last = is_last(t)
                with pe.Fori(2, Q_NEXT) as q:
                    pair(t, q)
                pair(t, 6)
                pair(t, 7)
                if not last:
                    pair(t, 8, 0)
                    pair(t, 9, 2)
                else:
                    _, (_, _, w), (_, _, _, u) = numbers(t, 7)
                    expert_up(TILES * E - 1, w + 1, E - 1)
                    pe.wait_ge(s_hid, w + 2)
                    turn(u + 1, hid)
                    expert_down(u + 1, E - 1)
                    pe.wait_ge(s_yz, t + 1)
                    turn(u + 2, yz)
                    head_first(t, w + 2, u + 2)
                    head_turn(t, u + 3)
                    head_second(u + 3)

            with pe.Fori(0, TILES - 1) as t:
                tile(t)
            tile(TILES - 1)

        @block.scalar
        def _(act):
            af = nc.scalar.activation
            act.wait_ge(s_w, W_ALL)
            act.wait_ge(s_pm, 1)
            af(pe_sb[:, :], banks[0][0:E, 0:D], ACT.Exp, bias=pe_st[:, 0:1],
               accum_out=pe_st[:, 1:2]).then_inc(s_px, 1)

            def copy_pv(n, g):
                act.wait_ge(sa_pv, n * 3 + (g + 1))
                af(qT[:, g, :], banks[1 + g][:, 0:SEQ], ACT.Copy).then_inc(sa_oq, 1)

            def image(n):
                act.wait_ge(sa_t, n + 1)
                af(a_xT[0:DC, :, :].rearrange("p c s -> p (c s)"), banks[1][0:DC, 0:2 * SEQ],
                   ACT.Copy).then_inc(sa_xT, 1)
                for g in range(3):
                    act.wait_ge(sa_q, n * 3 + (g + 1))
                    af(kT[:, g, :], banks[2 + g][:, SEQ:2 * SEQ], ACT.Identity,
                       bias=b_qk[:, 1, g:g + 1]).then_inc(sa_k, 1)
                for h in range(HEADS):
                    act.wait_ge(sa_s2, n * HEADS + (h + 1))
                    if h >= 8:
                        act.wait_ge(sa_pv, n * 3 + 1)
                    af(eT[:, h % 8, :, :].rearrange("p j s -> p (j s)"), banks[4 + h % 4][0:HALF, 0:2 * SEQ],
                       ACT.Exp, bias=1.0).then_inc(sa_e, 1)
                copy_pv(n, 0)
                copy_pv(n, 1)
                copy_pv(n, 2)
                act.wait_ge(sa_ot, n + 1)
                af(oT[0:DC, :, :].rearrange("p c s -> p (c s)"), banks[2][0:DC, 0:2 * SEQ],
                   ACT.Copy).then_inc(sa_oT, 1)

            with act.Fori(0, IMAGES) as n:
                image(n)

            def turned(no, dst, scale=1.0):
                act.wait_ge(s_tn, no + 1)
                af(dst[0:DC, :, :].rearrange("p c s -> p (c s)"), banks[5][0:DC, 0:256], ACT.Copy,
                   scale=scale).then_inc(s_hT, 1)

            def gate(P, par):
                act.wait_ge(s_g, P + 1)
                act.wait_ge(s_gu, P + 1)
                af(gs[:, par, :, :].rearrange("p a d -> p (a d)"), banks[0][:, 0:2 * D],
                   ACT.Copy).then_inc(s_gs, 1)

            def exps(P, par):
                act.wait_ge(s_so, P + 1)
                af(nmax[:, :, :].rearrange("p e o -> p (e o)"), vals[:, par, :, 0], ACT.Copy,
                   scale=-1.0).then_inc(ach, 1)
                act.wait_ge(ach, 1)
                act.wait_ge(s_wn, P * 2)
                for e in range(2):
                    af(ex[:, e, :], vals[:, par, e, :], ACT.Exp, bias=nmax[:, e, :],
                       accum_out=exs[:, e, :]).then_inc(s_ex, 1)

            def squares(P):
                act.wait_ge(s_h, P + 1)
                af(ab[64:128, 0, :, :], hf[0:64, :, :], ACT.Copy).then_inc(s_ab, 1)
                af(ab[64:128, 1, :, :], hf[64:128, :, :], ACT.Copy).then_inc(s_ab, 1)
                af(ab[0:64, 1, :, :], hf[64:128, :, :], ACT.Square).then_inc(s_ab, 1)

            def index_turned(P, par):
                act.wait_ge(s_wt, P + 1)
                act.wait_ge(s_mk, P)
                af(lT[:, :, :].rearrange("p e t -> p (e t)"), banks[0][0:K, 384:512].bitcast(BF16),
                   ACT.Copy).then_inc(s_lT, 1)
                af(wT[:, par, :, :].rearrange("p e t -> p (e t)"), banks[0][0:K, 0:256],
                   ACT.Copy).then_inc(s_wT, 1)

            def onehots(P, j):
                act.wait_ge(s_sp, P * 2 * CHUNKS + (j + 1))
                if j >= 4:
                    act.wait_ge(s_z, P * 2 * CHUNKS + (j - 3))
                af(onehot[:, j % 4, :, :].rearrange("p i k -> p (i k)"), banks[1 + j % 2][:, 0:CHUNK * K],
                   ACT.Relu, bias=hrow[:, :]).then_inc(s_oh, 1)

            def copy_candidates(P, j):
                e, c = j // CHUNKS, j % CHUNKS
                act.wait_ge(s_z, P * 2 * CHUNKS + (j + 1))
                act.wait_ge(s_pk, P * 2 * CHUNKS)
                af(zc[:, e, :, CT * c:CT * c + CT].rearrange("p l t -> p t l"),
                   banks[3 + j % 2][0:K, 0:CT * GL].rearrange("p (t l) -> p t l", l=GL),
                   ACT.Copy).then_inc(s_zc, 1)

            def gated(w):
                act.wait_ge(s_e, w + 1)
                act.wait_ge(s_hid, w)
                af(th[:, :], banks[6][:, 0:D], ACT.Tanh, scale=0.5).then_inc(s_th, 1)
                af(uh[:, :], banks[6][:, D:2 * D], ACT.Copy, scale=0.5).then_inc(s_u, 1)

            def head_tanh(t):
                act.wait_ge(s_m, t * 2 + 1)
                af(th[:, :], banks[6][:, 0:D], ACT.Tanh, scale=0.5).then_inc(s_mt, 1)

            def pair(t, q, par):
                P, (wx, wc, wo), (ux, uc, um, uo) = numbers(t, q)
                qi = q if isinstance(q, int) else None
                first_pair = t is None and q == 0
                halves = qi in (6, 7)
                head_2 = qi == Q_HEAD + 1
                act.sem_clear(ach)
                exps(P, par)
                squares(P)
                if halves:
                    gated(wx)
                elif head_2:
                    head_tanh(t)
                elif not first_pair:
                    gated(wc)
                index_turned(P, par)
                onehots(P, 0)
                onehots(P, 1)
                for j in range(2 * CHUNKS):
                    if j + 2 < 2 * CHUNKS:
                        onehots(P, j + 2)
                    copy_candidates(P, j)
                    if j == 1:
                        if halves:
                            turned(ux, hT)
                            gated(wc)
                        elif head_2:
                            turned(ux, hT, scale=0.5)
                        elif not first_pair:
                            turned(uc, hT)
                    if j == 3 and head_2:
                        gated(wc)
                    if j == 4 and halves:
                        turned(uc, hT)
                    if j == 4 and qi == Q_NEXT:
                        af(xS[:, :, :], xT[0:DC, :, :], ACT.Copy).then_inc(s_xS, 1)
                    if j == 5 and head_2:
                        turned(uc, hT)
                    if j == 5 and qi == Q_NEXT and not is_last(t):
                        turned(um, xT)
                    if j == 6:
                        if qi == Q_HEAD:
                            turned(um, zT)
                        gated(wo)
                if not (is_last(t) and qi in (6, 7)):
                    gate(P + 2, par)
                turned(uo, hT)

            act.wait_ge(s_gw, 1)
            turned(0, xT)
            act.sem_inc(s_zc, 1)
            gate(0, 0)
            gate(1, 1)
            pair(None, 0, 0)
            pair(None, 1, 1)

            def tile(t):
                with act.Fori(1, Q_NEXT // 2) as i:
                    pair(t, i * 2, 0)
                    pair(t, i * 2 + 1, 1)
                pair(t, 6, 0)
                pair(t, 7, 1)
                if not is_last(t):
                    pair(t, 8, 0)
                    pair(t, 9, 1)
                else:
                    _, (_, _, w), (_, _, _, u) = numbers(t, 7)
                    gated(w + 1)
                    turned(u + 1, hT)
                    turned(u + 2, zT)
                    head_tanh(t)
                    turned(u + 3, hT, scale=0.5)

            with act.Fori(0, TILES - 1) as t:
                tile(t)
            tile(TILES - 1)

        @block.gpsimd
        def _(pool):
            pl = nc.gpsimd

            def start(s, value):
                pool.wait_ge(s, value)
                pool.sem_inc(pgo, 1)

            def indices(P, par):
                start(s_so, P + 1)
                pl.tensor_scalar(idf[:, :, :], idx[:, par, :, :], 1.0, None, ALU.mult).then_inc(pch, 1)
                pool.wait_ge(pch, 1)
                pl.tensor_scalar(hq[:, :, :], idf[:, :, :], 1.0 / GL, -(GL - 1) / (2.0 * GL),
                                 ALU.mult, ALU.add).then_inc(pch, 1)
                pool.wait_ge(pch, 2)
                start(s_ab, P * 3)
                pl.tensor_scalar(hf[:, :, :], hq[:, :, :], MAGIC, MAGIC, ALU.add,
                                 ALU.subtract).then_inc(s_h, 1)
                start(s_h, P + 1)
                pl.tensor_scalar(hl[:, :, :], hf[:, :, :], -float(GL), None, ALU.mult).then_inc(pch, 1)
                pool.wait_ge(pch, 3)
                pool.wait_ge(s_wt, P)
                pl.tensor_tensor(lb[:, :, :], hl[:, :, :], idf[:, :, :], ALU.add).then_inc(s_l, 1)
                pool.wait_ge(s_sp, P * 2 * CHUNKS)
                pl.tensor_tensor(ab[0:64, 0, :, :], hf[0:64, :, :], hf[0:64, :, :], ALU.mult).then_inc(s_aq, 1)

            def pick(P, j):
                e, c = j // CHUNKS, j % CHUNKS
                pool.wait_ge(s_zc, P * 2 * CHUNKS + (j + 2))
                pool.wait_ge(s_ga, P * 2)
                pl.tensor_tensor(picked[:, e, :, CT * c:CT * c + CT], zc[:, e, :, CT * c:CT * c + CT],
                                 mask[:, :, e, CT * c:CT * c + CT], ALU.mult).then_inc(s_pk, 1)

            def hidden(w, no):
                pool.wait_ge(s_sg, w + 1)
                pool.wait_ge(s_u, w + 1)
                pool.wait_ge(s_tn, no)
                pl.tensor_tensor(hid[:, :], sg[:, :], uh[:, :], ALU.mult).then_inc(s_hid, 1)

            def pair(t, q, par):
                P, (wx, wc, wo), (ux, uc, um, uo) = numbers(t, q)
                qi = q if isinstance(q, int) else None
                pool.sem_clear(pch)
                indices(P, par)
                halves = qi in (6, 7)
                if halves:
                    hidden(wx, ux)
                elif qi != Q_HEAD + 1 and not (t is None and q == 0):
                    hidden(wc, uc)
                if qi == Q_NEXT and not is_last(t):
                    rstd(s_mv, t + 2, b_rs[:, :], b_mv[:, 1:2], 1e-5, s_rs)
                pool.wait_ge(s_mk, P + 1)
                for j in range(2 * CHUNKS):
                    pick(P, j)
                    if j == 3 and halves:
                        hidden(wc, uc)
                    if j == 4 and qi == Q_HEAD + 1:
                        hidden(wc, uc)
                    if j == Y_RSTD and qi == Q_HEAD:
                        rstd(s_ymv, t + 1, y_rs[:, :], y_mv[:, 1:2], 1e-6, s_yrs)
                    if j == OWN_HID:
                        hidden(wo, uo)

            OWN_HID = 7
            Y_RSTD = 3

            pl.memset(half_neg[:, :], -0.5).then_inc(s_hn, 1)
            pool.wait_ge(s_hn, 1)

            def rstd(ready, count, dst, var, eps, made):
                start(ready, count)
                pool.sem_clear(s_ve)
                pl.tensor_scalar(dst, var, eps, None, ALU.add).then_inc(s_ve, 1)
                pool.wait_ge(s_ve, 1)
                pl.tensor_tensor(dst, dst, half_neg[0:dst.shape[0], 0:dst.shape[1]], ALU.pow).then_inc(made, 1)

            with pool.Fori(0, IMAGES) as n:
                rstd(sa_mv, n * 2 + 2, a_rs[:, :, 0], a_mv[:, :, 1], 1e-5, sa_rs)
            rstd(s_mv, 1, b_rs[:, :], b_mv[:, 1:2], 1e-5, s_rs)

            pair(None, 0, 0)
            pair(None, 1, 1)

            def tile(t):
                with pool.Fori(1, Q_NEXT // 2) as i:
                    pair(t, i * 2, 0)
                    pair(t, i * 2 + 1, 1)
                pair(t, 6, 0)
                pair(t, 7, 1)
                if not is_last(t):
                    pair(t, 8, 0)
                    pair(t, 9, 1)
                else:
                    _, (_, _, w), (_, _, _, u) = numbers(t, 7)
                    hidden(w + 1, u + 1)
                    rstd(s_ymv, t + 1, y_rs[:, :], y_mv[:, 1:2], 1e-6, s_yrs)

            with pool.Fori(0, TILES - 1) as t:
                tile(t)
            tile(TILES - 1)

        @block.vector
        def _(dve):
            ve = nc.vector
            made = [0]

            def link(ins):
                made[0] += 1
                ins.then_inc(dch, 1)
                dve.wait_ge(dch, made[0])

            def new_chain():
                made[0] = 0
                dve.sem_clear(dch)

            def start(s, value):
                dve.wait_ge(s, value)
                dve.sem_inc(dgo, 1)

            link(ve.memset(xbd[:, :, :, :], 0.0))
            link(ve.memset(ones[:, :], 1.0))
            link(ve.memset(a_xT[DC:DC + 1, 0, :], 1.0))
            link(ve.memset(oT[DC:DC + 1, 0, :], 1.0))
            link(ve.memset(xT[DC:DC + 1, 0, :], 1.0))
            link(ve.memset(vaug[:, :, :, :], 0.0))
            link(ve.memset(vaug[:, :, :, HD:HD + 1], 1.0))
            link(ve.memset(mpad[:, :, :, :], 0.0))
            dve.wait_ge(s_w, W_ALL)
            link(ve.tensor_copy(identb[:, :], ident[:, :]))
            ve.tensor_copy(spread[:, :, :].rearrange("p g c -> p (g c)"), spread32[:, :]).then_inc(s_c, 1)
            dve.wait_ge(s_pp, 1)
            link(ve.tensor_reduce(pe_st[:, 2:3], banks[0][0:E, 0:D], AX_X, ALU.max))
            ve.tensor_scalar(pe_st[:, 0:1], pe_st[:, 2:3], -1.0, None, ALU.mult).then_inc(s_pm, 1)
            dve.wait_ge(s_px, 1)
            link(ve.reciprocal(pe_st[:, 3:4], pe_st[:, 1:2]))
            ve.tensor_scalar(pe_sb[:, :], pe_sb[:, :], pe_st[:, 3:4], None, ALU.mult).then_inc(s_pn, 1)
            dve.wait_ge(s_pt, 1)
            link(ve.tensor_copy(peT[:, :, :].rearrange("p c e -> p (c e)"), banks[2][0:DC, 0:2 * E]))
            for i in range(E):
                for c in range(2):
                    link(ve.tensor_scalar(gates[0:DC, c, i, :], gatew[:, c, :], peT[:, c, i:i + 1], None, ALU.mult))
            dve.wait_ge(s_lb, 1)
            link(ve.tensor_copy(mb[:, 0, :], banks[1][0:1, 0:D]))
            for c in range(2):
                link(ve.tensor_scalar(m1[:, c, :], m1[:, c, :], lngb[:, 0, c:c + 1], None, ALU.mult))
            dve.sem_inc(s_gw, 1)

            def image(n):
                new_chain()
                dve.wait_ge(sa_h, n + 1)
                link(ve.tensor_copy(h_sb[:, :, :].rearrange("p j d -> p (j d)"), banks[0][0:HALF, 0:2 * D]))
                for j in range(2):
                    link(ve.bn_stats(a_st[:, j, :], h_sb[:, j, :]))
                    ve.bn_aggr(a_mv[:, j, :], a_st[:, j, :]).then_inc(sa_mv, 1)
                dve.wait_ge(sa_rs, n + 1)
                for j in range(2):
                    ve.tensor_scalar(a_x[:, j, :], h_sb[:, j, :], a_mv[:, j, 0:1], a_rs[:, j, :],
                                     ALU.subtract, ALU.mult).then_inc(sa_x, 1)
                for g in range(3):
                    dve.wait_ge(sa_qk, n * 3 + (g + 1))
                    ve.tensor_scalar(qT[:, g, :], banks[2 + g][:, 0:SEQ], b_qk[:, 0, g:g + 1], HD ** -0.5,
                                     ALU.add, ALU.mult).then_inc(sa_q, 1)
                dve.wait_ge(sa_v, n + 1)
                ve.tensor_copy(vaug[:, :, :, 0:HD], banks[0][0:HALF, 0:2 * D].rearrange(
                    "p (j h d) -> p j h d", j=2, h=HEADS)).then_inc(sa_va, 1)
                for h in range(HEADS):
                    dve.wait_ge(sa_s, n * HEADS + (h + 1))
                    ve.tensor_reduce(mx[:, :, h:h + 1], banks[4 + h % 4][0:HALF, 0:2 * SEQ].rearrange(
                        "p (j s) -> p j s", j=2), AX_X, ALU.max).then_inc(sa_mx, 1)
                dve.wait_ge(sa_mx, n * HEADS + HEADS)
                ve.tensor_scalar(mpad[:, :, :, HD:HD + 1], mx[:, :, :].rearrange("p j (h o) -> p j h o", o=1),
                                 -1.0, -1.0, ALU.mult, ALU.add).then_inc(sa_mp, 1)
                dve.wait_ge(sa_mt, n + 1)
                ve.tensor_tensor(q2T[:, 0:2, :].rearrange("p g s -> p (g s)"), banks[2][:, 0:2 * SEQ],
                                 qT[:, 0:2, :].rearrange("p g s -> p (g s)"), ALU.add).then_inc(sa_q2, 1)
                ve.tensor_tensor(q2T[:, 2, :], banks[3][:, 0:SEQ], qT[:, 2, :], ALU.add).then_inc(sa_q2, 1)
                for j in range(2):
                    dve.wait_ge(sa_ob, n * 2 + (j + 1))
                    ov = banks[4 + j][0:HALF, 0:HEADS * 32].rearrange("p (h w) -> p h w", w=32)
                    link(ve.reciprocal(rc[:, j, :].rearrange("p (h o) -> p h o", o=1), ov[:, :, HD:HD + 1]))
                    ve.tensor_tensor(o_sb[:, j, :].rearrange("p (h d) -> p h d", d=HD), ov[:, :, 0:HD],
                                     rc[:, j, :].rearrange("p (h o) -> p h o", o=1).broadcast_to(
                                         [HALF, HEADS, HD]), ALU.mult).then_inc(sa_o, 1)
                dve.wait_ge(sa_y, n + 1)
                dve.wait_ge(s_h1, n * 16)
                ve.tensor_tensor(hout[:, :, :].rearrange("p j d -> p (j d)"), banks[0][0:HALF, 0:2 * D],
                                 h_sb[:, :, :].rearrange("p j d -> p (j d)"), ALU.add).then_inc(sa_out, 1)

            with dve.Fori(0, IMAGES) as n:
                image(n)

            def tile_stats(t):
                dve.wait_ge(s_ht, (t + 1) * 16)
                link(ve.bn_stats(b_st[:, :], ht[:, :]))
                ve.bn_aggr(b_mv[:, :], b_st[:, :]).then_inc(s_mv, 1)

            def normalise(t):
                if not isinstance(t, int) or t > 0:
                    dve.wait_ge(s_xs, t * 16)
                dve.wait_ge(s_rs, t + 1)
                ve.tensor_scalar(xn[:, :], ht[:, :], b_mv[:, 0:1], b_rs[:, :],
                                 ALU.subtract, ALU.mult).then_inc(s_xn, 1)

            def weigh(P):
                dve.wait_ge(s_ex, P * 2 + 2)
                link(ve.reciprocal(exr[:, :, 0], exs[:, :, 0]))
                dve.wait_ge(s_wt, P)
                for e in range(2):
                    ve.tensor_scalar(wn[:, e, :], ex[:, e, :], exr[:, e, :], None, ALU.mult).then_inc(s_wn, 1)

            def masks(P):
                dve.wait_ge(s_lT, P + 1)
                dve.wait_ge(s_pk, P * 2 * CHUNKS)
                for l in range(GL):
                    ins = ve.tensor_scalar(mask[:, l, :, :], lT[:, :, :], float(l), None, ALU.is_equal)
                ins.then_inc(s_mk, 1)

            def gathered(n, e, par):
                dve.wait_ge(s_ga, n + 1)
                ve.tensor_tensor(gw[:, :], banks[6][0:K, 2 * D:2 * D + 128], wT[:, par, e, :], ALU.mult).then_inc(s_gx, 1)

            def silu(w):
                dve.wait_ge(s_u, w + 1)
                dve.wait_ge(s_hid, w)
                ve.scalar_tensor_tensor(sg[:, :], th[:, :], 1.0, banks[6][:, 0:D], ALU.add,
                                        ALU.mult).then_inc(s_sg, 1)

            def sort(P, par, slots):
                new_chain()
                base = 0
                start(s_gs, P + 1)
                for r in range(ROUNDS):
                    src = [gs[:, par, e, :] if r == 0 else left[:, e, :] for e in range(2)]
                    v = [vals[:, par, e, 8 * r:8 * r + 8] for e in range(2)]
                    for e in range(2):
                        if r:
                            dve.wait_ge(dch, replaced - 1 + e)
                        ve.max(v[e], src[e]).then_inc(dch, 1)
                    for e in range(2):
                        dve.wait_ge(dch, base + 1 + e)
                        ve.max_index(idx[:, par, e, 8 * r:8 * r + 8], v[e], src[e]).then_inc(dch, 1)
                    if r < ROUNDS - 1:
                        for e in range(2):
                            ins = ve.match_replace(left[:, e, :], v[e], src[e], LOW).then_inc(dch, 1)
                        base += 6
                        if r == 0:
                            dve.wait_ge(dch, base)
                            dve.sem_inc(s_gu, 1)
                    else:
                        base += 4
                        dve.wait_ge(dch, base)
                        dve.sem_inc(s_so, 1)
                    made[0] = base
                    replaced = base
                    for f in slots.get(r, ()):
                        f()
                    base = made[0]

            GATHER1, WEIGH, SILU1, MASKS, GATHER0, SILU0 = 1, 1, 2, 2, 8, 10
            SH, SH_MASKS, SH_SILU1, SH_GATHER0, SH_SILU0, STATS, NORM = 3, 2, 6, 10, 11, 3, 5
            HID, H_MASKS, OUT, H_SILU1, H_GATHER0, H_SILU0 = 3, 2, 6, 8, 11, 11
            Y_STATS, Y_NORM = 6, 8

            def after(t, q, par):
                P, (wx, wc, wo), _ = numbers(t, q)
                n0 = P * 2
                masks_at, silu1_at, gather0_at, silu0_at = MASKS, SILU1, GATHER0, SILU0
                jobs = []
                if not (t is None and q == 0):
                    jobs.append((GATHER1, lambda: gathered(n0 - 1, 1, 1 - par)))
                jobs.append((WEIGH, lambda: weigh(P)))
                if isinstance(q, int) and t is not None:
                    if q in (6, 7):
                        masks_at, silu1_at, gather0_at, silu0_at = SH_MASKS, SH_SILU1, SH_GATHER0, SH_SILU0
                        jobs.append((SH, lambda: silu(wx)))
                    if q == Q_NEXT and not is_last(t):
                        jobs += [(STATS, lambda: tile_stats(t + 1)), (NORM, lambda: normalise(t + 1))]
                    if q == Q_HEAD:
                        jobs += [(Y_STATS, lambda: y_stats(t, wc + 1)), (Y_NORM, lambda: y_normalise(t))]
                    if q == Q_HEAD + 1:
                        masks_at, silu1_at, gather0_at, silu0_at = H_MASKS, H_SILU1, H_GATHER0, H_SILU0
                        jobs += [(HID, lambda: head_hidden(t, wc)), (OUT, lambda: head_out(t))]
                if not (t is None and q == 0):
                    jobs.append((silu1_at, lambda: silu(wc)))
                jobs += [(masks_at, lambda: masks(P)),
                         (gather0_at, lambda: gathered(n0, 0, par)), (silu0_at, lambda: silu(wo))]
                slots = {}
                for r, job in sorted(jobs, key=lambda x: x[0]):
                    slots.setdefault(r, []).append(job)
                return slots

            def y_stats(t, w):
                dve.wait_ge(s_dn, w)
                link(ve.bn_stats(y_st[:, :], banks[7][:, 0:D]))
                ve.bn_aggr(y_mv[:, :], y_st[:, :]).then_inc(s_ymv, 1)

            def y_normalise(t):
                dve.wait_ge(s_yrs, t + 1)
                ve.tensor_scalar(yz[:, :], banks[7][:, 0:D], y_mv[:, 0:1], y_rs[:, :],
                                 ALU.subtract, ALU.mult).then_inc(s_yz, 1)

            def head_hidden(t, w):
                dve.wait_ge(s_mt, t + 1)
                dve.wait_ge(s_hid, w)
                ve.scalar_tensor_tensor(hid[:, :], th[:, :], 1.0, banks[6][:, 0:D], ALU.add,
                                        ALU.mult).then_inc(s_mh, 1)

            def head_out(t):
                dve.wait_ge(s_m, t * 2 + 2)
                dve.wait_ge(s_res, (t + 1) * 16)
                dve.wait_ge(s_st, t * 16)
                ve.tensor_tensor(ot[:, :], banks[6][:, D:2 * D], hres[:, :], ALU.add).then_inc(s_of, 1)

            new_chain()
            dve.sem_inc(s_gu, 2)
            tile_stats(0)
            normalise(0)
            sort(0, 0, {})
            sort(1, 1, after(None, 0, 0))
            sort(2, 0, after(None, 1, 1))

            def tile(t):
                P = t * PAIRS
                with dve.Fori(1, Q_NEXT // 2) as i:
                    sort(P + i * 2 + 1, 1, after(t, i * 2, 0))
                    sort(P + i * 2 + 2, 0, after(t, i * 2 + 1, 1))
                sort(P + 7, 1, after(t, 6, 0))
                if not is_last(t):
                    sort(P + 8, 0, after(t, 7, 1))
                    sort(P + 9, 1, after(t, 8, 0))
                    sort(P + 10, 0, after(t, 9, 1))
                else:
                    slots = after(t, 7, 1)
                    for r in sorted(slots):
                        for f in slots[r]:
                            f()
                    w = numbers(t, 7)[1][2]
                    gathered(TILES * E - 1, 1, 1)
                    silu(w + 1)
                    y_stats(t, w + 2)
                    y_normalise(t)
                    head_hidden(t, w + 2)
                    head_out(t)

            with dve.Fori(0, TILES - 1) as t:
                tile(t)
            tile(TILES - 1)


def kernel(x, cls_tok, **w):
    import concourse.bacc as bacc
    from concourse.bass_utils import run_bass_kernel_spmd

    def c(v):
        return np.ascontiguousarray(np.asarray(v))

    def chunked(v):
        v = np.asarray(v)
        return v.reshape((v.shape[0] // DC, DC) + v.shape[1:]).swapaxes(0, 1)

    def row(v):
        return np.asarray(v).reshape(1, D)

    t = {k[3:]: np.asarray(v) for k, v in w.items()}
    ident, spread, hrow, sel = constants()
    x = np.asarray(x).reshape(IMAGES, 3, 14, 16, 14, 16).transpose(0, 1, 3, 5, 2, 4).reshape(
        IMAGES, PK, 128, 196)
    xp = np.zeros((IMAGES, 128, PK, SEQ), np.float32)
    xp[:, :, :, 2:] = x.transpose(0, 2, 1, 3)
    wqkv, bqkv = t["attn_w_qkv"].reshape(3, HEADS, HD, D), t["attn_b_qkv"].reshape(3, HEADS, HD)
    wqk = np.zeros((2, HEADS, 32, D), np.float32)
    wqk[:, :, :HD] = wqkv[:2]
    bqk = np.zeros((2, HEADS, 32), np.float32)
    bqk[:, :, :HD] = bqkv[:2]
    bqk[1, :, HD] = 1.0
    arrays = {
        "x": xp, "ident": ident, "spread": spread, "hrow": hrow, "sel": sel,
        "cls_tok": row(cls_tok), "tok_cls": row(t["tok_cls_token"]), "tok_b": row(t["tok_b_lin"]),
        "w_patch": t["tok_W_lin"].T.reshape(PK, 128, D).transpose(1, 0, 2),
        "w_qk": chunked(wqk.reshape(2, 3, 128, D).transpose(3, 0, 1, 2)),
        "b_qk": bqk.reshape(2, 3, 128).transpose(2, 0, 1),
        "w_v": chunked(wqkv[2].reshape(D, D).T), "b_v": row(bqkv[2]),
        "w_o": chunked(t["attn_w_out"].T), "b_o": row(t["attn_b_out"]),
        "gate_w": chunked(t["ffn_gate_w"]), "gate_b": row(t["ffn_gate_b"]),
        "eg_w": t["ffn_eg_w"].transpose(1, 0, 2), "eu_w": t["ffn_eu_w"].transpose(1, 0, 2),
        "ed_w": t["ffn_ed_w"].reshape(E, 2, DC, D).transpose(2, 1, 0, 3),
        "sg_w": chunked(t["ffn_sg_w"].reshape(D, 2, D)), "su_w": chunked(t["ffn_su_w"].reshape(D, 2, D)),
        "sd_w": t["ffn_sd_w"].reshape(2, 2, DC, D).transpose(2, 0, 1, 3),
        "m1_w": chunked(t["ffn_m1_w"]), "m2_w": chunked(t["ffn_m2_w"]),
        "m1_b": row(t["ffn_m1_b"]), "m2_b": row(t["ffn_m2_b"]),
        "ln_g": chunked(t["ffn_ln_g"]), "ln_b": chunked(t["ffn_ln_b"]),
        "posT": chunked(t["ffn_posembed"].T), "pos_w": chunked(t["ffn_pos_w"]), "pos_b": row(t["ffn_pos_b"]),
    }
    nc = bacc.Bacc("TRN2", target_bir_lowering=False, num_devices=1)
    ins, aps = {}, {}
    for name, v in arrays.items():
        v = c(v)
        ins[f"in_{name}"] = v
        aps[name] = nc.dram_tensor(f"in_{name}", v.shape, mybir.dt.from_np(v.dtype), kind="ExternalInput").ap()
    out = nc.dram_tensor("out", (TOKENS, D), F32, kind="ExternalOutput").ap()
    build(nc, aps, out)
    r = run_bass_kernel_spmd(nc, [ins], core_ids=[0])
    return r.results[0]["out"].reshape(IMAGES, SEQ, D)
```
